# Optimizing a Trainium2 kernel written in Bass

```python
import numpy as np
import jax
import jax.numpy as jnp

def _softmax(x, axis=-1):
    return jax.nn.softmax(x, axis=axis)

def _gelu(x):
    return jax.nn.gelu(x, approximate=True)

def _silu(x):
    return jax.nn.silu(x)

def _sigmoid(x):
    return jax.nn.sigmoid(x)

def _layernorm(x, axis=-1, eps=1e-05):
    m = jnp.mean(x, axis=axis, keepdims=True)
    v = jnp.var(x, axis=axis, keepdims=True)
    return (x - m) / jnp.sqrt(v + eps)

def _scatter_add(tgt, idx, src, axis=0):
    return tgt.at[idx].add(src)

def _segment_sum(src, seg, n):
    return jax.ops.segment_sum(src, seg, n)
kernel_name = 'mk_adj_resnorm_d2_adj_r2_9f2fad'

def setup_inputs(seed: int=0):
    np.random.seed(seed)
    _w = jnp.asarray

    def _rec_inputs():
        import jax
        import jax.numpy as jnp
        _gk = jax.random.key(seed)
        x = -0.001547 + 1.001 * jax.random.normal(jax.random.fold_in(_gk, 1), (64, 128, 128), jnp.float32)
        _a = jax.random.bernoulli(jax.random.fold_in(_gk, 2), 0.015625, (64, 128, 128))
        _a = jnp.logical_or(_a, jnp.swapaxes(_a, -1, -2))
        _a = jnp.logical_or(_a, jnp.eye(128, dtype=bool))
        _af = _a.astype(jnp.float32)
        _af = _af * jax.random.uniform(jax.random.fold_in(_gk, 3), (64, 128, 128), jnp.float32, 0.05, 4.99997)
        adj = _af
        return (x, adj)
    x, adj = _rec_inputs()

    def _L0_gnn_setup():
        import jax, jax.numpy as jnp
        import numpy as np
        B, N, NAB, NF, NG = (8, 128, 128, 128, 64)
        CUTOFF = 5.0
        LN2 = float(np.log(2.0))

        def ssp(x):
            return jax.nn.softplus(x) - LN2
        key = jax.random.key(seed)
        ks = jax.random.split(key, 12)
        r = jax.random.normal(ks[0], (B, N, NAB), dtype=jnp.float32)
        e = jax.random.uniform(ks[1], (B, N, N), dtype=jnp.float32) * CUTOFF
        A = (jax.random.uniform(ks[2], (B, N, N)) < 0.3).astype(jnp.float32)
        s = 0.05
        W1 = jax.random.normal(ks[3], (NF, NG), dtype=jnp.float32) * s
        b1 = jnp.zeros((NF,), jnp.float32)
        W2 = jax.random.normal(ks[4], (NF, NF), dtype=jnp.float32) * s
        b2 = jnp.zeros((NF,), jnp.float32)
        Wa = jax.random.normal(ks[5], (NF, NAB), dtype=jnp.float32) * s
        Wd1 = jax.random.normal(ks[6], (NAB, NF), dtype=jnp.float32) * s
        bd1 = jnp.zeros((NAB,), jnp.float32)
        Wd2 = jax.random.normal(ks[7], (NAB, NAB), dtype=jnp.float32) * s
        bd2 = jnp.zeros((NAB,), jnp.float32)
        return {'r': r, 'e': e, 'A': A, 'W1': W1, 'b1': b1, 'W2': W2, 'b2': b2, 'Wa': Wa, 'Wd1': Wd1, 'bd1': bd1, 'Wd2': Wd2, 'bd2': bd2}
    _L0_gnn_all = _L0_gnn_setup()
    _L0_gnn_in = {k: v for k, v in _L0_gnn_all.items() if k in ('W1', 'b1', 'W2', 'b2', 'Wa', 'Wd1', 'bd1', 'Wd2', 'bd2')}
    del _L0_gnn_all

    def _L1_gnn_setup():
        import jax, jax.numpy as jnp
        import numpy as np
        key = jax.random.key(seed)
        k1, k2, k3 = jax.random.split(key, 3)
        B, N, Din, Dout = (8, 2048, 128, 128)
        x = jax.random.normal(k1, (B, N, Din), dtype=jnp.float32)
        adj = jax.random.uniform(k2, (B, N, N), dtype=jnp.float32)
        limit = float(np.sqrt(6.0 / (Din + Dout)))
        weight = jax.random.uniform(k3, (Din, Dout), dtype=jnp.float32, minval=-limit, maxval=limit)
        bias = jnp.zeros((Dout,), dtype=jnp.float32)
        return {'x': x, 'adj': adj, 'weight': weight, 'bias': bias}
    _L1_gnn_all = _L1_gnn_setup()
    _L1_gnn_in = {k: v for k, v in _L1_gnn_all.items() if k in ('weight', 'bias')}
    del _L1_gnn_all
    return {'x': x, 'adj': adj, 'L0_gnn_W1': _L0_gnn_in['W1'], 'L0_gnn_b1': _L0_gnn_in['b1'], 'L0_gnn_W2': _L0_gnn_in['W2'], 'L0_gnn_b2': _L0_gnn_in['b2'], 'L0_gnn_Wa': _L0_gnn_in['Wa'], 'L0_gnn_Wd1': _L0_gnn_in['Wd1'], 'L0_gnn_bd1': _L0_gnn_in['bd1'], 'L0_gnn_Wd2': _L0_gnn_in['Wd2'], 'L0_gnn_bd2': _L0_gnn_in['bd2'], 'L1_gnn_weight': _L1_gnn_in['weight'], 'L1_gnn_bias': _L1_gnn_in['bias']}

def reference(x, adj, L0_gnn_W1, L0_gnn_b1, L0_gnn_W2, L0_gnn_b2, L0_gnn_Wa, L0_gnn_Wd1, L0_gnn_bd1, L0_gnn_Wd2, L0_gnn_bd2, L1_gnn_weight, L1_gnn_bias):
    import jax
    import jax.numpy as jnp

    def _L0_gnn_ref(r, e, A, W1, b1, W2, b2, Wa, Wd1, bd1, Wd2, bd2):
        import jax, jax.numpy as jnp
        import numpy as np
        B, N, NAB, NF, NG = (8, 128, 128, 128, 64)
        CUTOFF = 5.0
        LN2 = float(np.log(2.0))

        def ssp(x):
            return jax.nn.softplus(x) - LN2
        offsets = jnp.linspace(0.0, CUTOFF, NG, dtype=jnp.float32)
        width = offsets[1] - offsets[0]
        coeff = -0.5 / (width * width)
        diff = e[:, :, :, None] - offsets
        g = jnp.exp(coeff * diff * diff)
        h = ssp(jnp.einsum('bijg,fg->bijf', g, W1) + b1)
        Wf = jnp.einsum('bijf,gf->bijg', h, W2) + b2
        rf = jnp.einsum('bjd,fd->bjf', r, Wa)
        Am = A[:, :, :, None]
        Wf = Wf * Am
        y = jnp.einsum('bjf,bijf->bif', rf, Wf * Am)
        y = ssp(jnp.einsum('bif,df->bid', y, Wd1) + bd1)
        y = jnp.einsum('bid,ed->bie', y, Wd2) + bd2
        return y

    def _L1_gnn_ref(x, adj, weight, bias):
        import jax, jax.numpy as jnp
        import numpy as np
        B, N, _ = x.shape
        adj = adj + jnp.eye(N, dtype=adj.dtype)[None]
        degree = adj.sum(axis=2)
        d_inv_sqrt = degree ** (-0.5)
        d_inv_sqrt = jnp.where(jnp.isinf(d_inv_sqrt), 0.0, d_inv_sqrt)
        adj_norm = d_inv_sqrt[:, :, None] * adj * d_inv_sqrt[:, None, :]
        support = jnp.einsum('bnd,de->bne', x, weight)
        out = jnp.einsum('bnm,bme->bne', adj_norm, support) + bias
        return out
    x = _layernorm(x + _L0_gnn_ref(x, adj, adj, L0_gnn_W1, L0_gnn_b1, L0_gnn_W2, L0_gnn_b2, L0_gnn_Wa, L0_gnn_Wd1, L0_gnn_bd1, L0_gnn_Wd2, L0_gnn_bd2), axis=-1)
    x = _layernorm(x + _L1_gnn_ref(x, adj, L1_gnn_weight, L1_gnn_bias), axis=-1)
    return x

_drawn_inputs = setup_inputs


def setup_inputs(seed=0):
    import zlib

    import numpy as np

    out = dict(_drawn_inputs(seed))
    spreads = {'L0_gnn_b1': (0.0, 0.1),
     'L0_gnn_b2': (0.0, 0.1),
     'L0_gnn_bd1': (0.0, 0.1),
     'L0_gnn_bd2': (0.0, 0.1),
     'L1_gnn_bias': (0.0, 0.1)}
    factors = {}
    for name, (base, spread) in spreads.items():
        noise = np.random.default_rng([zlib.crc32(name.encode()), seed]).standard_normal(out[name].shape)
        drawn = base * np.exp(spread * noise) if base else spread * noise
        out[name] = jnp.asarray(drawn.astype(out[name].dtype))
    for name, factor in factors.items():
        out[name] = (out[name] * factor).astype(out[name].dtype)
    return out
```

```python
import math
from collections import namedtuple
from contextlib import ExitStack

import numpy as np

import concourse.bass as bass
from concourse import mybir

B, P, NG = 64, 128, 64
CUTOFF = 5.0
LN2 = math.log(2.0)
EPS = 1e-5
GRAPHS = 4
GROUPS = B // GRAPHS
TOP = 8
PAIRS = TOP // 2
W = GRAPHS * P
BLOCK = P // GRAPHS
SAFE = 30.0

PREP_DVE = ["top", "differ", "edge", "hi", "rest", "mid", "lo", "square",
            "left", "top2", "differ2", "edge2", "count"]
PAIR_PE = ["base", "rows", "edge", "lin1", "lin2", "left", "rf", "y"]
PAIR_DVE = ["end", "from", "pick", "rank", "edge", "hi", "rest", "mid", "lo", "hot", "msg"]
PAIR_ACT = ["square", "gauss", "exp", "soft", "filter"]
TAIL_PE = ["degree", "lin1", "lin2", "spread", "out"]
TAIL_DVE = ["degree", "clamp", "soft", "sum1", "stats1", "moments1", "var1", "norm1",
            "sum2", "stats2", "moments2", "var2", "norm2"]
TAIL_ACT = ["exp", "log", "spread"]
TAIL_POOL = ["base", "root", "power", "dinv", "rstd1", "scaled", "biased", "rstd2"]
DENSE_PE = ["turn", "edge", "lin1", "lin2", "y"]
DENSE_DVE = ["hi", "rest", "mid", "lo", "clamp", "soft", "shift", "msg", "y"]
DENSE_ACT = ["turn", "square", "gauss", "exp", "log"]

Group = namedtuple("Group", "n half h")


def at(names, n, name):
    return n * len(names) + names.index(name) + 1


def wait(eng, sem, value):
    if not isinstance(value, int) or value > 0:
        eng.wait_ge(sem, value)


def gnn_kernel(nc, adjT, x, xT, w1T, b1, w2T, b2, waT, wd1T, bd1, wd2T, bd2, wg, bg, w1, offsets, out,
               force_dense=False, dense_groups=GROUPS):
    f32, bf16, i32 = mybir.dt.float32, mybir.dt.bfloat16, mybir.dt.int32
    ALU, ACT, AX = mybir.AluOpType, mybir.ActivationFunctionType, mybir.AxisListType
    width = np.linspace(0.0, CUTOFF, NG, dtype=np.float32)
    width = np.float32(width[1] - width[0])
    COEFF = float(np.float32(-0.5) / (width * width))

    with ExitStack() as ctx:
        def sb(name, shape, dt=f32):
            return ctx.enter_context(nc.sbuf_tensor(name, shape, dt))

        def pb(name):
            return ctx.enter_context(nc.psum_tensor(name, [P, W], f32))

        def sem(name):
            return ctx.enter_context(nc.semaphore(name))

        W1T, W2T, WAT = sb("W1T", [P, P]), sb("W2T", [P, P]), sb("WAT", [P, P])
        WD1T, WD2T, WG = sb("WD1T", [P, P]), sb("WD2T", [P, P]), sb("WG", [P, P])
        W1 = sb("W1", [P, NG])
        cols = sb("cols", [P, 8])
        B1, BD1, NOFF = cols[:, 0:1], cols[:, 1:2], cols[:, 2:3]
        B1L, BD1L, BOUND, B1ABS, POS = cols[:, 3:4], cols[:, 4:5], cols[:, 5:6], cols[:, 6:7], cols[:, 7:8]
        B2R, BD2R, BGR = sb("B2R", [P, P]), sb("BD2R", [P, P]), sb("BGR", [P, P])
        ident, identb = sb("ident", [P, P]), sb("identb", [P, P], bf16)
        before, iota = sb("before", [P, P]), sb("iota", [P, P])
        ones, minus_half = sb("ones", [P, 1]), sb("minus_half", [P, GRAPHS])
        w1abs = sb("w1abs", [P, NG])
        halfc = sb("halfc", [P, 1])

        A = [sb(f"A{h}", [P, GRAPHS, P]) for h in (0, 1)]
        XT = [sb(f"XT{h}", [P, GRAPHS, P]) for h in (0, 1)]
        XN = sb("XN", [P, GRAPHS, P])
        top = [sb(f"top{h}", [P, GRAPHS, TOP]) for h in (0, 1)]
        differ = sb("differ", [P, GRAPHS, TOP])
        edge = [sb(f"edge{h}", [P, GRAPHS, TOP]) for h in (0, 1)]
        rest = sb("rest", [P, GRAPHS, TOP])
        packed = [sb(f"packed{h}", [P, GRAPHS, BLOCK], bf16) for h in (0, 1)]
        parts = [[packed[h][:, :, i * TOP:(i + 1) * TOP] for i in range(3)] for h in (0, 1)]
        turned = sb("turned", [P, P], bf16)
        choose = sb("choose", [P, GRAPHS, PAIRS, P], bf16)
        square = [sb(f"square{h}", [P, GRAPHS, TOP]) for h in (0, 1)]
        left = [sb(f"left{h}", [P, GRAPHS, P]) for h in (0, 1)]
        top2, differ2 = sb("top2", [P, TOP]), sb("differ2", [P, TOP])
        lane = sb("lane", [P, TOP + 1])
        count, junk8 = sb("count", [P, 1]), sb("junk8", [P, TOP])
        flags = sb("flags", [P, 4])
        least, unused = sb("least", [P, 1]), sb("unused", [P, GRAPHS, P])
        RF = [sb(f"RF{h}", [P, GRAPHS, P]) for h in (0, 1)]
        RFB = sb("RFB", [P, GRAPHS, P])
        A2 = [sb(f"A2{h}", [P, GRAPHS, P]) for h in (0, 1)]
        AI = [sb(f"AI{h}", [P, GRAPHS, P]) for h in (0, 1)]
        hot = [sb(f"hot{h}", [P, TOP, P]) for h in (0, 1)]
        DIFF2, G = sb("DIFF2", [P, PAIRS, P]), sb("G", [P, PAIRS, P])
        EX = [sb(f"EX{i}", [P, PAIRS, P]) for i in (0, 1)]
        H = [sb(f"H{i}", [P, PAIRS, P]) for i in (0, 1)]
        Z = [sb(f"Z{i}", [P, PAIRS, P]) for i in (0, 1)]
        span_end, started, pick = sb("span_end", [P, 1]), sb("started", [P, P]), sb("pick", [P, P])
        e2 = sb("e2", [P, 4])
        place, E2, E2R, E2SQ = e2[:, 0:1], e2[:, 1:2], e2[:, 2:3], e2[:, 3:4]
        parts2 = [sb(f"parts2{i}", [P, 1], bf16) for i in range(3)]
        junk2 = sb("junk2", [P, TOP])
        D2, G2, EX2, H2, WF2 = (sb(n, [P, P]) for n in ("D2", "G2", "EX2", "H2", "WF2"))
        hot2, Z2 = sb("hot2", [P, GRAPHS, P]), sb("Z2", [P, GRAPHS, P])
        YS, UC, S1 = (sb(n, [P, GRAPHS, P]) for n in ("YS", "UC", "S1"))
        UE, UL, XB, R1, X1 = (sb(n, [P, GRAPHS, P]) for n in ("UE", "UL", "XB", "R1", "X1"))
        XS, X1B, SP, R2 = (sb(n, [P, GRAPHS, P]) for n in ("XS", "X1B", "SP", "R2"))
        OUT = sb("OUT", [P, GRAPHS, P])
        deg = sb("deg", [P, 5, GRAPHS])
        DEG0, DEG1, DEGN, ROOT, DINV = (deg[:, i, :] for i in range(5))
        stats = sb("stats", [P, GRAPHS, 6])
        mv = [sb(f"mv{i}", [P, GRAPHS, 2]) for i in (0, 1)]
        var = [sb(f"var{i}", [P, GRAPHS]) for i in (0, 1)]
        rstd = [sb(f"rstd{i}", [P, GRAPHS]) for i in (0, 1)]
        spare = sb("spare", [P, 1])
        worst, bad, verdict = sb("worst", [P, 1]), sb("bad", [P, 1]), sb("verdict", [1, 1], i32)
        VB, VR = sb("VB", [P, TOP]), sb("VR", [P, TOP])

        pE, pX0, pX1, pW0, pW1, pY, pM0, pM1 = (pb(n) for n in ("pE", "pX0", "pX1", "pW0", "pW1", "pY", "pM0", "pM1"))

        s_const, s_setup = sem("consts_loaded"), sem("consts_made")
        s_A = [sem(f"adj_loaded{h}") for h in (0, 1)]
        s_XT = [sem(f"xT_loaded{h}") for h in (0, 1)]
        s_XN, s_out = sem("x_loaded"), sem("out_stored")
        pe_e, pe_x = sem("edges_spread"), [sem(f"lin1_done{i}") for i in (0, 1)]
        pe_w, pe_s = [sem(f"filter_done{i}") for i in (0, 1)], [sem(f"summed{i}") for i in (0, 1)]
        act_e, act_g = sem("diff_squared"), sem("gauss_done")
        act_x, act_h = [sem(f"exp_done{i}") for i in (0, 1)], [sem(f"soft_done{i}") for i in (0, 1)]
        dve_hot, dve_z = sem("hot_done"), [sem(f"message_done{i}") for i in (0, 1)]
        dve_prep, pe_rf, act_rf = sem("prep_dve"), sem("rf_done"), sem("rf_copied")
        pe_turn, act_turned = sem("parts_turned"), sem("turned_copied")
        pool_sq, pool_rfb, pool_ai = sem("squares_done"), sem("rfb_done"), sem("adj_eye_done")
        act_least, dve_least = sem("negatives_summed"), sem("negatives_noted")
        pe_pair, dve_pair, act_pair = sem("pair_pe"), sem("pair_dve"), sem("pair_act")
        act_y = sem("y_copied")
        pe_tail, dve_tail, act_tail, pool_tail = sem("tail_pe"), sem("tail_dve"), sem("tail_act"), sem("tail_pool")
        s_verdict, s_count, s_bound, s_pool = sem("verdict"), sem("bad_counted"), sem("bound_done"), sem("pool_consts")
        d_in, d_block, d_store = sem("dense_in"), sem("dense_block"), sem("dense_stored")
        dn_pe, dn_dve, dn_act = sem("dense_pe"), sem("dense_dve"), sem("dense_act")
        dn_rf, dn_rfc, dn_ai, dn_free = sem("dense_rf"), sem("dense_rf_copied"), sem("dense_adj_eye"), sem("dense_block_free")

        block = ctx.enter_context(nc.Block())

        def run(body):
            def step(n, half, h, first=False, last=False):
                g = Group(n, half, h)
                nxt = None if last else Group(n + 1, half + h, 1 - h)
                prev = None if first else Group(n - 1, half - 1 + h, 1 - h)
                body(g, nxt, prev)
            return step

        def groups(eng, body):
            step = run(body)
            step(0, 0, 0, first=True)
            step(1, 0, 1)
            with eng.Fori(0, GROUPS // 2 - 2) as t:
                step(2 * t + 2, t + 1, 0)
                step(2 * t + 3, t + 1, 1)
            step(GROUPS - 2, GROUPS // 2 - 1, 0)
            step(GROUPS - 1, GROUPS // 2 - 1, 1, last=True)
            body(None, None, Group(GROUPS - 1, GROUPS // 2 - 1, 1))

        CONSTS = [(W1T[0:NG, :], w1T), (W1T[NG:P, :], w1T), (W2T[:, :], w2T), (WAT[:, :], waT), (WD1T[:, :], wd1T),
                  (WD2T[:, :], wd2T), (WG[:, :], wg), (W1[:, :], w1), (B1, b1), (BD1, bd1), (NOFF, offsets),
                  (B2R[:, :], b2.broadcast_to([P, P])), (BD2R[:, :], bd2.broadcast_to([P, P])),
                  (BGR[:, :], bg.broadcast_to([P, P]))]

        @block.sync
        def _(eng):
            def load_adj(g, n, half):
                eng.dma_start(A[g.h][:, :, :], adjT[:, bass.ds(n * W, W)]).then_inc(s_A[g.h], 16)

            def load_xT(g, n):
                eng.dma_start(XT[g.h][:, :, :], xT[:, bass.ds(n * W, W)]).then_inc(s_XT[g.h], 16)

            def body(g, nxt, prev):
                if g:
                    n = g.n
                    static = isinstance(n, int)
                    more = not static or n + 2 < GROUPS
                    if more:
                        wait(eng, pe_rf, n + 1)
                        load_xT(g, n + 2)
                    if prev:
                        wait(eng, pool_tail, at(TAIL_POOL, n - 1, "base"))
                    eng.dma_start(XN[:, :, :], x[:, bass.ds(n * W, W)]).then_inc(s_XN, 16)
                    if more:
                        wait(eng, dve_hot, GRAPHS * (n + 1))
                        wait(eng, pool_ai, n + 1)
                        wait(eng, act_least, n + 1)
                        load_adj(g, n + 2, None)
                if prev:
                    c = prev.n
                    wait(eng, dve_tail, at(TAIL_DVE, c, "norm2"))
                    eng.dma_start(out[:, bass.ds(c * W, W)], OUT[:, :, :]).then_inc(s_out, 16)

            load_adj(Group(0, 0, 0), 0, 0)
            load_xT(Group(0, 0, 0), 0)
            for dst, src in CONSTS:
                eng.dma_start(dst, src).then_inc(s_const, 16)
            load_adj(Group(1, 0, 1), 1, 0)
            load_xT(Group(1, 0, 1), 1)
            groups(eng, body)
            eng.wait_ge(s_out, 16 * GROUPS)

            eng.wait_ge(s_verdict, 1)
            flagged = eng.value_load(verdict[0:1, 0:1])
            with eng.If(flagged != 0):
                with eng.Fori(0, dense_groups) as n:
                    eng.dma_start(A[0][:, :, :], adjT[:, bass.ds(n * W, W)]).then_inc(d_in, 16)
                    eng.dma_start(XT[0][:, :, :], xT[:, bass.ds(n * W, W)]).then_inc(d_in, 16)
                    eng.dma_start(XN[:, :, :], x[:, bass.ds(n * W, W)]).then_inc(d_in, 16)
                    with eng.Fori(0, GRAPHS) as q:
                        with eng.Fori(0, P // TOP) as t:
                            k = (n * GRAPHS + q) * (P // TOP) + t
                            eng.dma_start(VB[:, :], adjT[:, bass.ds(n * W + q * P + t * TOP, TOP)]).then_inc(d_block, 16)
                            eng.wait_ge(dn_dve, (k + 1) * len(DENSE_DVE))
                            eng.sem_inc(dn_free, 1)
                    eng.wait_ge(dve_tail, at(TAIL_DVE, n + GROUPS, "norm2"))
                    eng.dma_start(out[:, bass.ds(n * W, W)], OUT[:, :, :]).then_inc(d_store, 16)
                    eng.wait_ge(d_store, 16 * (n + 1))
                    eng.sem_inc(dn_free, 1)

        def tail_pe(eng, c, n, h, stage):
            if stage == "degree":
                if h is None:
                    eng.wait_ge(dn_ai, c - GROUPS + 1)
                else:
                    eng.wait_ge(pool_ai, c + 1)
                wait(eng, dve_tail, at(TAIL_DVE, c - 1, "sum2"))
                if h is not None:
                    eng.wait_ge(act_turned, min(c + 2, GROUPS) if isinstance(c, int) else c + 2)
                for q in range(GRAPHS):
                    last = eng.matmul(pM0[:, q:q + 1], AI[h or 0][:, q, :], ones[:, :], start=True, stop=True)
                last.then_inc(pe_tail, 1)
            if stage == "lin1":
                eng.wait_ge(act_y, c + 1)
                eng.wait_ge(dve_tail, at(TAIL_DVE, c, "degree"))
                eng.matmul(pM0[:, :], WD1T[:, :], YS[:, :, :], start=True, stop=True).then_inc(pe_tail, 1)
            if stage == "lin2":
                eng.wait_ge(dve_tail, at(TAIL_DVE, c, "soft"))
                for q in range(GRAPHS):
                    last = eng.matmul(pM0[:, bass.ts(q, P)], S1[:, q, :], WD2T[:, :], start=True, stop=True)
                last.then_inc(pe_tail, 1)
            if stage == "spread":
                eng.wait_ge(pool_tail, at(TAIL_POOL, c, "scaled"))
                if h is not None:
                    eng.wait_ge(act_turned, min(c + 3, GROUPS) if isinstance(c, int) else c + 3)
                for q in range(GRAPHS):
                    last = eng.matmul(pM0[:, bass.ts(q, P)], XS[:, q, :], AI[h or 0][:, q, :], start=True, stop=True)
                last.then_inc(pe_tail, 1)
            if stage == "out":
                eng.wait_ge(act_tail, at(TAIL_ACT, c, "spread"))
                for q in range(GRAPHS):
                    last = eng.matmul(pM0[:, bass.ts(q, P)], SP[:, q, :], WG[:, :], start=True, stop=True)
                last.then_inc(pe_tail, 1)

        def tail_act(eng, c, stage):
            if stage == "soft":
                eng.wait_ge(dve_tail, at(TAIL_DVE, c, "clamp"))
                eng.activation(UE[:, :, :], UC[:, :, :], ACT.Exp).then_inc(act_tail, 1)
                eng.wait_ge(act_tail, at(TAIL_ACT, c, "exp"))
                eng.activation(UL[:, :, :], UE[:, :, :], ACT.Ln, bias=halfc[:, :], scale=0.5).then_inc(act_tail, 1)
            if stage == "spread":
                eng.wait_ge(pe_tail, at(TAIL_PE, c, "spread"))
                eng.activation(SP[:, :, :], pM0[:, :], ACT.Copy).then_inc(act_tail, 1)

        def layer_norm_stats(eng, c, i, R):
            eng.wait_ge(dve_tail, at(TAIL_DVE, c, f"sum{i + 1}"))
            for q in range(GRAPHS):
                last = eng.bn_stats(stats[:, q, :], R[:, q, :])
            last.then_inc(dve_tail, 1)
            eng.wait_ge(dve_tail, at(TAIL_DVE, c, f"stats{i + 1}"))
            eng.memset(spare[:, :], 0.0)
            for q in range(GRAPHS):
                last = eng.bn_aggr(mv[i][:, q, :], stats[:, q, :])
            last.then_inc(dve_tail, 1)
            eng.wait_ge(dve_tail, at(TAIL_DVE, c, f"moments{i + 1}"))
            eng.tensor_scalar(var[i][:, :], mv[i][:, :, 1], EPS, None, ALU.add).then_inc(dve_tail, 1)

        def layer_norm_apply(eng, c, i, R, to):
            eng.wait_ge(pool_tail, at(TAIL_POOL, c, f"rstd{i + 1}"))
            for q in range(GRAPHS):
                last = eng.tensor_scalar(to[:, q, :], R[:, q, :], mv[i][:, q, 0:1], rstd[i][:, q:q + 1],
                                         ALU.subtract, ALU.mult)
            last.then_inc(dve_tail, 1)

        def tail_dve(eng, c, stage):
            if stage == "degree":
                eng.wait_ge(pe_tail, at(TAIL_PE, c, "degree"))
                wait(eng, pool_tail, at(TAIL_POOL, c - 1, "rstd2"))
                eng.tensor_scalar(DEG0, pM0[:, 0:GRAPHS], 0.0, None, ALU.is_equal)
                eng.tensor_scalar(DEGN, pM0[:, 0:GRAPHS], 0.0, None, ALU.not_equal)
                eng.tensor_copy(DEG1, pM0[:, 0:GRAPHS]).then_inc(dve_tail, 1)
            if stage == "clamp":
                eng.wait_ge(pe_tail, at(TAIL_PE, c, "lin1"))
                eng.tensor_scalar(UC[:, :, :], pM0[:, :], BD1, SAFE, ALU.add, ALU.min).then_inc(dve_tail, 1)
            if stage == "soft":
                eng.wait_ge(act_tail, at(TAIL_ACT, c, "log"))
                eng.scalar_tensor_tensor(S1[:, :, :], pM0[:, :], BD1L, UL[:, :, :], ALU.add, ALU.max).then_inc(dve_tail, 1)
            if stage == "sum1":
                eng.wait_ge(pe_tail, at(TAIL_PE, c, "lin2"))
                eng.wait_ge(pool_tail, at(TAIL_POOL, c, "base"))
                eng.tensor_tensor(R1[:, :, :], pM0[:, :], XB[:, :, :], ALU.add).then_inc(dve_tail, 1)
                layer_norm_stats(eng, c, 0, R1)
            if stage == "norm1":
                layer_norm_apply(eng, c, 0, R1, X1)
            if stage == "sum2":
                eng.wait_ge(pe_tail, at(TAIL_PE, c, "out"))
                eng.wait_ge(pool_tail, at(TAIL_POOL, c, "biased"))
                for q in range(GRAPHS):
                    last = eng.scalar_tensor_tensor(R2[:, q, :], pM0[:, bass.ts(q, P)], DINV[:, q:q + 1],
                                                    X1B[:, q, :], ALU.mult, ALU.add)
                last.then_inc(dve_tail, 1)
                layer_norm_stats(eng, c, 1, R2)
            if stage == "norm2":
                layer_norm_apply(eng, c, 1, R2, OUT)

        def tail_pool(eng, c, stage):
            if stage == "base":
                wait(eng, dve_tail, at(TAIL_DVE, c - 1, "sum1"))
                eng.tensor_tensor(XB[:, :, :], XN[:, :, :], BD2R[:, :].unsqueeze(1).broadcast_to([P, GRAPHS, P]),
                                  ALU.add).then_inc(pool_tail, 1)
            if stage == "dinv":
                eng.wait_ge(dve_tail, at(TAIL_DVE, c, "degree"))
                eng.tensor_tensor(ROOT, DEG1, DEG0, ALU.add).then_inc(pool_tail, 1)
                eng.wait_ge(pool_tail, at(TAIL_POOL, c, "root"))
                eng.tensor_tensor(ROOT, ROOT, minus_half[:, :], ALU.pow).then_inc(pool_tail, 1)
                eng.wait_ge(pool_tail, at(TAIL_POOL, c, "power"))
                eng.tensor_tensor(DINV, ROOT, DEGN, ALU.mult).then_inc(pool_tail, 1)
            if stage in ("rstd1", "rstd2"):
                i = int(stage[-1]) - 1
                eng.wait_ge(dve_tail, at(TAIL_DVE, c, f"var{i + 1}"))
                eng.tensor_tensor(rstd[i][:, :], var[i][:, :], minus_half[:, :], ALU.pow).then_inc(pool_tail, 1)
            if stage == "scaled":
                eng.wait_ge(dve_tail, at(TAIL_DVE, c, "norm1"))
                eng.tensor_tensor(XS[:, :, :], X1[:, :, :], DINV.unsqueeze(2).broadcast_to([P, GRAPHS, P]),
                                  ALU.mult).then_inc(pool_tail, 1)
                eng.tensor_tensor(X1B[:, :, :], X1[:, :, :], BGR[:, :].unsqueeze(1).broadcast_to([P, GRAPHS, P]),
                                  ALU.add).then_inc(pool_tail, 1)

        def spread_edges(eng, q):
            for p in range(PAIRS):
                last = eng.matmul(pE[:, bass.ts(p, P)], choose[:, q, p, :], turned[:, :], start=True, stop=True)
            return last

        @block.tensor
        def _(eng):
            def project(g):
                eng.wait_ge(s_XT[g.h], 16 * (g.half + 1))
                wait(eng, dve_pair, at(PAIR_DVE, g.n - 2, "msg"))
                for q in range(GRAPHS):
                    last = eng.matmul(pM1[:, bass.ts(q, P)], XT[g.h][:, q, :], WAT[:, :], start=True, stop=True)
                last.then_inc(pe_rf, 1)

            def spread(g, q):
                u = GRAPHS * g.n + q
                if q == 0:
                    eng.wait_ge(act_turned, g.n + 1)
                wait(eng, act_e, u)
                spread_edges(eng, q).then_inc(pe_e, 1)

            def turn(g, prev):
                eng.wait_ge(dve_prep, at(PREP_DVE, g.n, "lo"))
                if prev:
                    eng.wait_ge(dve_tail, at(TAIL_DVE, prev.n, "sum1"))
                eng.matmul(pM0[:, 0:P], packed[g.h][:, :, :], identb[:, :], start=True, stop=True).then_inc(pe_turn, 1)

            def lin1(g, q):
                u = GRAPHS * g.n + q
                eng.wait_ge(act_g, u + 1)
                wait(eng, act_x[0], u)
                wait(eng, act_x[1], u)
                eng.matmul(pX0[:, :], W1T[0:NG, :], G[0:NG, :, :], start=True, stop=True).then_inc(pe_x[0], 1)
                eng.matmul(pX1[:, :], W1T[NG:P, :], G[NG:P, :, :], start=True, stop=True).then_inc(pe_x[1], 1)

            def lin2(g, q, i):
                u = GRAPHS * g.n + q
                eng.wait_ge(act_h[i], u + 1)
                wait(eng, dve_z[i], u)
                for p in range(PAIRS):
                    last = eng.matmul((pW0, pW1)[i][:, bass.ts(p, P)], H[i][:, p, :], W2T[:, :], start=True, stop=True)
                last.then_inc(pe_w[i], 1)

            def messages(g, q, i):
                u = GRAPHS * g.n + q
                if i == 0:
                    if q == 0:
                        eng.wait_ge(pool_rfb, g.n + 1)
                        eng.wait_ge(pool_sq, g.n + 1)
                        wait(eng, act_y, g.n)
                    eng.matmul(pY[:, bass.ts(q, P)], RFB[:, q, :], A2[g.h][:, q, :], start=q == 0, stop=False,
                               skip_group_check=True)
                    eng.wait_ge(dve_hot, u + 1)
                eng.wait_ge(dve_z[i], u + 1)
                for p in range(PAIRS):
                    last = eng.matmul(pY[:, bass.ts(q, P)], Z[i][:, p, :], hot[q % 2][:, 2 * p + i, :],
                                      start=False, stop=False, skip_group_check=True)
                last.then_inc(pe_s[i], 1)

            def pair(g, stage):
                n = g.n
                if stage == "base":
                    eng.wait_ge(dve_prep, at(PREP_DVE, n, "count"))
                    eng.wait_ge(act_rf, min(n + 2, GROUPS) if isinstance(n, int) else n + 2)
                    eng.matmul(pM1[:, 0:1], before[:, :], count[:, :], start=True, stop=True).then_inc(pe_pair, 1)
                if stage == "rows":
                    eng.wait_ge(dve_pair, at(PAIR_DVE, n, "pick"))
                    eng.matmul(pM1[:, 0:TOP + 1], pick[:, :], lane[:, :], start=True, stop=True).then_inc(pe_pair, 1)
                if stage == "edge":
                    eng.wait_ge(dve_pair, at(PAIR_DVE, n, "lo"))
                    for i, part in enumerate(parts2):
                        last = eng.matmul(pM1[0:NG, 0:P], part[:, 0:1].broadcast_to([P, NG]), identb[:, :],
                                          start=i == 0, stop=i == 2)
                    last.then_inc(pe_pair, 1)
                if stage == "lin1":
                    eng.wait_ge(act_pair, at(PAIR_ACT, n, "gauss"))
                    eng.matmul(pM1[:, 0:P], W1T[0:NG, :], G2[0:NG, :], start=True, stop=True).then_inc(pe_pair, 1)
                if stage == "lin2":
                    eng.wait_ge(act_pair, at(PAIR_ACT, n, "soft"))
                    eng.matmul(pM1[:, 0:P], H2[:, :], W2T[:, :], start=True, stop=True).then_inc(pe_pair, 1)
                if stage == "left":
                    eng.wait_ge(act_pair, at(PAIR_ACT, n, "filter"))
                    eng.matmul(pM1[:, :], pick[:, :], left[g.h][:, :, :], start=True, stop=True).then_inc(pe_pair, 1)
                if stage == "rf":
                    eng.wait_ge(dve_pair, at(PAIR_DVE, n, "hot"))
                    eng.matmul(pM1[:, :], pick[:, :], RF[g.h][:, :, :], start=True, stop=True).then_inc(pe_pair, 1)
                if stage == "y":
                    eng.wait_ge(dve_pair, at(PAIR_DVE, n, "msg"))
                    for q in range(GRAPHS):
                        last = eng.matmul(pY[:, bass.ts(q, P)], Z2[:, q, :], hot2[:, q, :], start=False,
                                          stop=q == GRAPHS - 1, skip_group_check=True)
                    last.then_inc(pe_pair, 1)

            def body(g, nxt, prev):
                def tail(stage):
                    if prev:
                        tail_pe(eng, prev.n, prev.n, prev.h, stage)

                if not g:
                    for stage in TAIL_PE:
                        tail(stage)
                    return
                for q in range(GRAPHS):
                    after = (g, q + 1) if q + 1 < GRAPHS else (nxt, 0)
                    if q == 0:
                        if nxt:
                            project(nxt)
                        tail("degree")
                    if q == 1:
                        pair(g, "rows")
                    if q == 2:
                        pair(g, "lin1")
                        tail("lin2")
                    if q == 3:
                        pair(g, "left")
                        tail("spread")
                    lin2(g, q, 0)
                    if after[0]:
                        spread(*after)
                    lin2(g, q, 1)
                    messages(g, q, 0)
                    if q == 0:
                        pair(g, "base")
                        tail("lin1")
                    if q == 1:
                        pair(g, "edge")
                    if q == 2:
                        pair(g, "lin2")
                        if nxt:
                            turn(nxt, prev)
                    if q == 3:
                        pair(g, "rf")
                        tail("out")
                    if after[0]:
                        lin1(*after)
                    messages(g, q, 1)
                pair(g, "y")

            eng.wait_ge(s_const, 16 * len(CONSTS))
            eng.wait_ge(s_setup, 1)
            first = Group(0, 0, 0)
            project(first)
            turn(first, None)
            spread(first, 0)
            lin1(first, 0)
            groups(eng, body)

            eng.wait_ge(s_count, 1)
            eng.matmul(pM1[0:1, 0:1], bad[:, :], ones[:, :], start=True, stop=True).then_inc(s_count, 1)
            eng.wait_ge(s_verdict, 1)
            flagged = eng.value_load(verdict[0:1, 0:1])
            with eng.If(flagged != 0):
                with eng.Fori(0, dense_groups) as n:
                    eng.wait_ge(d_in, 48 * (n + 1))
                    for q in range(GRAPHS):
                        last = eng.matmul(pM1[:, bass.ts(q, P)], XT[0][:, q, :], WAT[:, :], start=True, stop=True)
                    last.then_inc(dn_rf, 1)
                    with eng.Fori(0, GRAPHS * P // TOP) as m:
                        k = n * (GRAPHS * P // TOP) + m
                        eng.wait_ge(dn_dve, at(DENSE_DVE, k, "lo"))
                        eng.matmul(pW0[:, 0:P], packed[0][:, :, :], identb[:, :], start=True, stop=True).then_inc(dn_pe, 1)
                        eng.wait_ge(dn_act, at(DENSE_ACT, k, "turn"))
                        spread_edges(eng, 0).then_inc(dn_pe, 1)
                        eng.wait_ge(dn_act, at(DENSE_ACT, k, "gauss"))
                        eng.matmul(pX0[:, :], W1T[0:NG, :], G[0:NG, :, :], start=True, stop=True)
                        eng.matmul(pX1[:, :], W1T[NG:P, :], G[NG:P, :, :], start=True, stop=True).then_inc(dn_pe, 1)
                        eng.wait_ge(dn_dve, at(DENSE_DVE, k, "soft"))
                        for i in (0, 1):
                            for p in range(PAIRS):
                                last = eng.matmul((pW0, pW1)[i][:, bass.ts(p, P)], H[i][:, p, :], W2T[:, :],
                                                  start=True, stop=True)
                        last.then_inc(dn_pe, 1)
                        eng.wait_ge(dn_dve, at(DENSE_DVE, k, "msg"))
                        for s in range(TOP):
                            last = eng.matmul(pY[:, s:s + 1], Z[s % 2][:, s // 2, :], square[0][:, 0, s:s + 1],
                                              start=True, stop=True)
                        last.then_inc(dn_pe, 1)
                    for stage in TAIL_PE:
                        tail_pe(eng, n + GROUPS, n, None, stage)

        @block.scalar
        def _(eng):
            def squares(g, q):
                u = GRAPHS * g.n + q
                eng.wait_ge(pe_e, u + 1)
                eng.activation(DIFF2[:, :, :], pE[:, :], ACT.Square, bias=NOFF).then_inc(act_e, 1)
                eng.wait_ge(act_e, u + 1)
                wait(eng, pe_x[1], u)
                eng.activation(G[:, :, :], DIFF2[:, :, :], ACT.Exp, scale=COEFF).then_inc(act_g, 1)

            def soft(g, q, i):
                u = GRAPHS * g.n + q
                eng.wait_ge(pe_x[i], u + 1)
                eng.activation(EX[i][:, :, :], (pX0, pX1)[i][:, :], ACT.Exp, bias=B1).then_inc(act_x[i], 1)
                eng.wait_ge(act_x[i], u + 1)
                wait(eng, pe_w[i], u)
                eng.activation(H[i][:, :, :], EX[i][:, :, :], ACT.Ln, bias=halfc[:, :], scale=0.5).then_inc(act_h[i], 1)

            def copy_rf(g):
                eng.wait_ge(pe_rf, g.n + 1)
                wait(eng, pe_pair, at(PAIR_PE, g.n - 2, "rf"))
                wait(eng, dve_z[1], GRAPHS * (g.n - 1))
                wait(eng, pool_rfb, g.n - 1)
                eng.activation(RF[g.h][:, :, :], pM1[:, :], ACT.Copy).then_inc(act_rf, 1)

            def copy_turned(g):
                eng.wait_ge(pe_turn, g.n + 1)
                eng.activation(turned[:, :], pM0[:, 0:P], ACT.Copy).then_inc(act_turned, 1)

            def copy_y(g):
                eng.wait_ge(pe_pair, at(PAIR_PE, g.n, "y"))
                wait(eng, pe_tail, at(TAIL_PE, g.n - 1, "lin1"))
                eng.activation(YS[:, :, :], pY[:, :], ACT.Copy).then_inc(act_y, 1)

            def pair_gauss(g):
                eng.wait_ge(pe_pair, at(PAIR_PE, g.n, "edge"))
                eng.activation(D2[0:NG, :], pM1[0:NG, 0:P], ACT.Square, bias=NOFF[0:NG, :]).then_inc(act_pair, 1)
                eng.wait_ge(act_pair, at(PAIR_ACT, g.n, "square"))
                eng.activation(G2[0:NG, :], D2[0:NG, :], ACT.Exp, scale=COEFF).then_inc(act_pair, 1)

            def pair_soft(g):
                eng.wait_ge(pe_pair, at(PAIR_PE, g.n, "lin1"))
                eng.activation(EX2[:, :], pM1[:, 0:P], ACT.Exp, bias=B1).then_inc(act_pair, 1)
                eng.wait_ge(act_pair, at(PAIR_ACT, g.n, "exp"))
                eng.activation(H2[:, :], EX2[:, :], ACT.Ln, bias=halfc[:, :], scale=0.5).then_inc(act_pair, 1)

            def pair_filter(g):
                eng.wait_ge(pe_pair, at(PAIR_PE, g.n, "lin2"))
                wait(eng, dve_pair, at(PAIR_DVE, g.n - 1, "msg"))
                eng.activation(WF2[:, :], pM1[:, 0:P], ACT.Copy).then_inc(act_pair, 1)

            def negatives(g):
                eng.wait_ge(s_A[g.h], 16 * (g.half + 1))
                wait(eng, dve_least, g.n)
                eng.activation(unused[:, :, :], A[g.h][:, :, :], ACT.Relu, scale=-1.0, accum_out=least[:, :])\
                   .then_inc(act_least, 1)

            def body(g, nxt, prev):
                if prev:
                    copy_y(prev)
                if not g:
                    for stage in ("soft", "spread"):
                        tail_act(eng, prev.n, stage)
                    return
                for q in range(GRAPHS):
                    after = (g, q + 1) if q + 1 < GRAPHS else (nxt, 0)
                    soft(g, q, 0)
                    if q == 0 and nxt:
                        copy_rf(nxt)
                    if q == 2:
                        pair_soft(g)
                    if q == 3 and prev:
                        tail_act(eng, prev.n, "spread")
                    soft(g, q, 1)
                    if after[0]:
                        squares(*after)
                    if q == 1:
                        if prev:
                            tail_act(eng, prev.n, "soft")
                        pair_gauss(g)
                    if q == 0:
                        negatives(g)
                    if q == 2:
                        pair_filter(g)
                        if nxt:
                            copy_turned(nxt)

            eng.preload_act_table_set("natural_log_exp_and_others")
            eng.wait_ge(s_const, 16 * len(CONSTS))
            eng.wait_ge(s_setup, 1)
            first = Group(0, 0, 0)
            copy_rf(first)
            copy_turned(first)
            squares(first, 0)
            groups(eng, body)

            eng.wait_ge(s_verdict, 1)
            flagged = eng.value_load(verdict[0:1, 0:1])
            with eng.If(flagged != 0):
                with eng.Fori(0, dense_groups) as n:
                    eng.wait_ge(dn_rf, n + 1)
                    eng.activation(RF[0][:, :, :], pM1[:, :], ACT.Copy).then_inc(dn_rfc, 1)
                    with eng.Fori(0, GRAPHS * P // TOP) as m:
                        k = n * (GRAPHS * P // TOP) + m
                        eng.wait_ge(dn_pe, at(DENSE_PE, k, "turn"))
                        eng.activation(turned[:, :], pW0[:, 0:P], ACT.Copy).then_inc(dn_act, 1)
                        eng.wait_ge(dn_pe, at(DENSE_PE, k, "edge"))
                        eng.activation(DIFF2[:, :, :], pE[:, :], ACT.Square, bias=NOFF).then_inc(dn_act, 1)
                        eng.wait_ge(dn_act, at(DENSE_ACT, k, "square"))
                        eng.activation(G[:, :, :], DIFF2[:, :, :], ACT.Exp, scale=COEFF).then_inc(dn_act, 1)
                        eng.wait_ge(dn_dve, at(DENSE_DVE, k, "clamp"))
                        for i in (0, 1):
                            last = eng.activation(H[i][:, :, :], EX[i][:, :, :], ACT.Exp)
                        last.then_inc(dn_act, 1)
                        eng.wait_ge(dn_act, at(DENSE_ACT, k, "exp"))
                        for i in (0, 1):
                            last = eng.activation(EX[i][:, :, :], H[i][:, :, :], ACT.Ln, bias=halfc[:, :], scale=0.5)
                        last.then_inc(dn_act, 1)
                    for stage in ("soft", "spread"):
                        tail_act(eng, n + GROUPS, stage)

        @block.vector
        def _(eng):
            def parts_of(value, exact, left_over, sem_, names, k):
                eng.tensor_copy(exact[0], value).then_inc(sem_, 1)
                eng.wait_ge(sem_, at(names, k, "hi"))
                eng.tensor_tensor(left_over, value, exact[0], ALU.subtract).then_inc(sem_, 1)
                eng.wait_ge(sem_, at(names, k, "rest"))
                eng.tensor_copy(exact[1], left_over).then_inc(sem_, 1)
                eng.wait_ge(sem_, at(names, k, "mid"))
                eng.tensor_tensor(exact[2], left_over, exact[1], ALU.subtract).then_inc(sem_, 1)

            def prep_top(g):
                eng.wait_ge(s_A[g.h], 16 * (g.half + 1))
                eng.memset(spare[:, :], 0.0)
                for q in range(GRAPHS):
                    last = eng.max(top[g.h][:, q, :], A[g.h][:, q, :])
                last.then_inc(dve_prep, 1)

            def prep_parts(g):
                n, h = g.n, g.h
                eng.wait_ge(dve_prep, at(PREP_DVE, n, "top"))
                eng.tensor_tensor(differ[:, :, 1:TOP], top[h][:, :, 1:TOP], top[h][:, :, 0:TOP - 1],
                                  ALU.not_equal).then_inc(dve_prep, 1)
                eng.wait_ge(dve_prep, at(PREP_DVE, n, "differ"))
                eng.tensor_copy(edge[h][:, :, 0:1], top[h][:, :, 0:1])
                eng.tensor_tensor(edge[h][:, :, 1:TOP], top[h][:, :, 1:TOP], differ[:, :, 1:TOP],
                                  ALU.mult).then_inc(dve_prep, 1)
                eng.wait_ge(dve_prep, at(PREP_DVE, n, "edge"))
                wait(eng, pe_turn, n - 1)
                parts_of(edge[h][:, :, :], parts[h], rest[:, :, :], dve_prep, PREP_DVE, n)
                eng.tensor_tensor(square[h][:, :, :], edge[h][:, :, :], edge[h][:, :, :], ALU.mult).then_inc(dve_prep, 1)

            def prep_left(g):
                n, h = g.n, g.h
                wait(eng, pe_pair, at(PAIR_PE, n - 2, "left"))
                for q in range(GRAPHS):
                    last = eng.scalar_tensor_tensor(left[h][:, q, :], A[h][:, q, :], top[h][:, q, TOP - 1:TOP],
                                                    A[h][:, q, :], ALU.is_lt, ALU.mult)
                last.then_inc(dve_prep, 1)
                eng.wait_ge(dve_prep, at(PREP_DVE, n, "left"))
                eng.memset(spare[:, :], 0.0)
                eng.max(top2[:, :], left[h][:, :, :]).then_inc(dve_prep, 1)
                eng.wait_ge(dve_prep, at(PREP_DVE, n, "top2"))
                eng.tensor_tensor(differ2[:, 1:TOP], top2[:, 1:TOP], top2[:, 0:TOP - 1], ALU.not_equal)\
                   .then_inc(dve_prep, 1)
                eng.tensor_tensor(flags[:, 0:1], flags[:, 0:1], top2[:, TOP - 1:TOP], ALU.max)
                eng.wait_ge(dve_prep, at(PREP_DVE, n, "differ2"))
                wait(eng, pe_pair, at(PAIR_PE, n - 1, "rows"))
                eng.tensor_copy(lane[:, 0:1], top2[:, 0:1])
                eng.tensor_tensor(lane[:, 1:TOP], top2[:, 1:TOP], differ2[:, 1:TOP], ALU.mult).then_inc(dve_prep, 1)
                eng.tensor_scalar(junk8[:, :], top2[:, :], 0.0, None, ALU.is_gt, ALU.add, accum_out=count[:, :])\
                   .then_inc(dve_prep, 1)

            def hots(g, q):
                u = GRAPHS * g.n + q
                if q == 0:
                    eng.wait_ge(dve_prep, at(PREP_DVE, g.n, "square"))
                wait(eng, pe_s[1], u - 1)
                for s in range(TOP):
                    last = eng.tensor_scalar(hot[q % 2][:, s, :], A[g.h][:, q, :], edge[g.h][:, q, s:s + 1],
                                             square[g.h][:, q, s:s + 1], ALU.is_equal, ALU.mult)
                last.then_inc(dve_hot, 1)

            def message(g, q, i):
                u = GRAPHS * g.n + q
                if q == 0 and i == 0:
                    eng.wait_ge(act_rf, g.n + 1)
                eng.wait_ge(pe_w[i], u + 1)
                wait(eng, pe_s[i], u)
                rf = RF[g.h][:, q, :].unsqueeze(1).broadcast_to([P, PAIRS, P])
                eng.tensor_tensor(Z[i][:, :, :], (pW0, pW1)[i][:, :].rearrange("p (a b) -> p a b", b=P), rf,
                                  ALU.mult).then_inc(dve_z[i], 1)

            def pair_pick(g):
                n = g.n
                eng.wait_ge(pe_pair, at(PAIR_PE, n, "base"))
                eng.tensor_copy(lane[:, TOP:TOP + 1], pM1[:, 0:1])
                eng.tensor_tensor(span_end[:, :], pM1[:, 0:1], count[:, :], ALU.add).then_inc(dve_pair, 1)
                eng.wait_ge(dve_pair, at(PAIR_DVE, n, "end"))
                eng.tensor_scalar(started[:, :], iota[:, :], lane[:, TOP:TOP + 1], None, ALU.is_ge)\
                   .then_inc(dve_pair, 1)
                eng.scalar_tensor_tensor(flags[:, 1:2], span_end[:, :], float(P), flags[:, 1:2],
                                         ALU.subtract, ALU.max)
                eng.wait_ge(dve_pair, at(PAIR_DVE, n, "from"))
                wait(eng, pe_pair, at(PAIR_PE, n - 1, "rf"))
                eng.scalar_tensor_tensor(pick[:, :], iota[:, :], span_end[:, :], started[:, :],
                                         ALU.is_lt, ALU.mult).then_inc(dve_pair, 1)

            def pair_edge(g):
                n = g.n
                eng.wait_ge(pe_pair, at(PAIR_PE, n, "rows"))
                eng.tensor_tensor(place, POS, pM1[:, TOP:TOP + 1], ALU.subtract).then_inc(dve_pair, 1)
                eng.wait_ge(dve_pair, at(PAIR_DVE, n, "rank"))
                eng.scalar_tensor_tensor(junk2[:, :], iota[:, 0:TOP], place, pM1[:, 0:TOP],
                                         ALU.is_equal, ALU.mult, accum_out=E2).then_inc(dve_pair, 1)
                eng.wait_ge(dve_pair, at(PAIR_DVE, n, "edge"))
                parts_of(E2, [x[:, :] for x in parts2], E2R, dve_pair, PAIR_DVE, n)
                eng.tensor_tensor(E2SQ, E2, E2, ALU.mult)

            def pair_hot(g):
                eng.wait_ge(pe_pair, at(PAIR_PE, g.n, "left"))
                wait(eng, pe_pair, at(PAIR_PE, g.n - 1, "y"))
                eng.tensor_scalar(hot2[:, :, :], pM1[:, :], E2, E2SQ, ALU.is_equal, ALU.mult).then_inc(dve_pair, 1)

            def pair_message(g):
                eng.wait_ge(pe_pair, at(PAIR_PE, g.n, "rf"))
                eng.tensor_tensor(Z2[:, :, :], pM1[:, :].rearrange("p (a b) -> p a b", b=P),
                                  WF2[:, :].unsqueeze(1).broadcast_to([P, GRAPHS, P]), ALU.mult).then_inc(dve_pair, 1)

            def least_seen(g):
                eng.wait_ge(act_least, g.n + 1)
                eng.tensor_tensor(flags[:, 2:3], flags[:, 2:3], least[:, :], ALU.max).then_inc(dve_least, 1)

            def body(g, nxt, prev):
                def tail(stage):
                    if prev:
                        if stage == "norm2":
                            wait(eng, s_out, 16 * prev.n)
                        tail_dve(eng, prev.n, stage)

                if not g:
                    for stage in ("degree", "clamp", "soft", "sum1", "norm1", "sum2", "norm2"):
                        tail(stage)
                    return
                for q in range(GRAPHS):
                    hots(g, q)
                    if q == 0:
                        tail("degree")
                    if q == 1:
                        pair_edge(g)
                    if q == 2:
                        tail("sum1")
                    message(g, q, 0)
                    if q == 1 and nxt:
                        prep_top(nxt)
                    if q == 2 and nxt:
                        prep_left(nxt)
                    if q == 3:
                        pair_hot(g)
                    message(g, q, 1)
                    if q == 0:
                        pair_pick(g)
                        tail("clamp")
                    if q == 1:
                        if nxt:
                            prep_parts(nxt)
                        tail("soft")
                    if q == 2:
                        tail("norm1")
                        least_seen(g)
                    if q == 3:
                        pair_message(g)
                        tail("sum2")
                        tail("norm2")

            eng.memset(flags[:, :], 0.0).then_inc(s_bound, 1)
            for h in (0, 1):
                last = eng.memset(packed[h][:, :, :], 0.0)
            last.then_inc(s_bound, 1)
            eng.wait_ge(s_bound, 2)
            eng.wait_ge(s_const, 16 * len(CONSTS))
            eng.tensor_scalar(cols[:, 3:5], cols[:, 0:2], -LN2, None, ALU.add)
            eng.scalar_tensor_tensor(w1abs[:, :], W1[:, :], -1.0, W1[:, :], ALU.mult, ALU.max)
            eng.scalar_tensor_tensor(B1ABS, B1, -1.0, B1, ALU.mult, ALU.max).then_inc(s_bound, 1)
            first = Group(0, 0, 0)
            prep_top(first)
            prep_parts(first)
            prep_left(first)
            eng.wait_ge(s_bound, 3)
            eng.reduce_sum(BOUND, w1abs[:, :], AX.X).then_inc(s_bound, 1)
            eng.wait_ge(s_bound, 4)
            eng.scalar_tensor_tensor(flags[:, 3:4], BOUND, -SAFE, B1ABS, ALU.add, ALU.add)
            groups(eng, body)

            eng.wait_ge(dve_least, GROUPS)
            eng.reduce_max(worst[:, :], flags[:, :], AX.X).then_inc(s_bound, 1)
            eng.wait_ge(s_bound, 5)
            eng.tensor_scalar(bad[:, :], worst[:, :], -1.0 if force_dense else 0.0, None, ALU.is_gt).then_inc(s_count, 1)
            eng.wait_ge(s_count, 2)
            eng.tensor_copy(verdict[:, :], pM1[0:1, 0:1]).then_inc(s_verdict, 1)
            eng.wait_ge(s_verdict, 1)
            flagged = eng.value_load(verdict[0:1, 0:1])
            with eng.If(flagged != 0):
                with eng.Fori(0, dense_groups) as n:
                    eng.wait_ge(dn_rfc, n + 1)
                    eng.memset(spare[:, :], 0.0)
                    with eng.Fori(0, GRAPHS) as q:
                        with eng.Fori(0, P // TOP) as t:
                            k = (n * GRAPHS + q) * (P // TOP) + t
                            eng.wait_ge(d_block, 16 * (k + 1))
                            eng.tensor_tensor(square[0][:, 0, :], VB[:, :], VB[:, :], ALU.mult)
                            parts_of(VB[:, :], [x[:, 0, :] for x in parts[0]], VR[:, :], dn_dve, DENSE_DVE, k)
                            eng.wait_ge(dn_pe, at(DENSE_PE, k, "lin1"))
                            for i, pX in enumerate((pX0, pX1)):
                                last = eng.tensor_scalar(EX[i][:, :, :], pX[:, :], B1, SAFE, ALU.add, ALU.min)
                            last.then_inc(dn_dve, 1)
                            eng.wait_ge(dn_act, at(DENSE_ACT, k, "log"))
                            for i, pX in enumerate((pX0, pX1)):
                                last = eng.scalar_tensor_tensor(H[i][:, :, :], pX[:, :], B1L, EX[i][:, :, :],
                                                                ALU.add, ALU.max)
                            last.then_inc(dn_dve, 1)
                            eng.wait_ge(dn_pe, at(DENSE_PE, k, "lin2"))
                            for i, pW in enumerate((pW0, pW1)):
                                last = eng.tensor_tensor(Z[i][:, :, :], pW[:, :].rearrange("p (a b) -> p a b", b=P),
                                                         B2R[:, :].unsqueeze(1).broadcast_to([P, PAIRS, P]), ALU.add)
                            last.then_inc(dn_dve, 1)
                            eng.wait_ge(dn_dve, at(DENSE_DVE, k, "shift"))
                            rf = RF[0].rearrange("p a b -> p (a b)")[:, bass.ds(q * P, P)]
                            for i in (0, 1):
                                last = eng.tensor_tensor(Z[i][:, :, :], Z[i][:, :, :],
                                                         rf.unsqueeze(1).broadcast_to([P, PAIRS, P]), ALU.mult)
                            last.then_inc(dn_dve, 1)
                            eng.wait_ge(dn_pe, at(DENSE_PE, k, "y"))
                            eng.tensor_copy(YS.rearrange("p a b -> p (a b)")[:, bass.ds(q * P + t * TOP, TOP)],
                                            pY[:, 0:TOP]).then_inc(dn_dve, 1)
                    eng.wait_ge(dn_dve, (n + 1) * (GRAPHS * P // TOP) * len(DENSE_DVE))
                    eng.sem_inc(act_y, 1)
                    for stage in ("degree", "clamp", "soft", "sum1", "norm1", "sum2", "norm2"):
                        tail_dve(eng, n + GROUPS, stage)

        @block.gpsimd
        def _(eng):
            def squares(g):
                eng.wait_ge(s_A[g.h], 16 * (g.half + 1))
                wait(eng, pe_s[0], GRAPHS * (g.n - 1))
                eng.tensor_tensor(A2[g.h][:, :, :], A[g.h][:, :, :], A[g.h][:, :, :], ALU.mult).then_inc(pool_sq, 1)

            def rfb(g):
                eng.wait_ge(act_rf, g.n + 1)
                wait(eng, pe_s[0], GRAPHS * g.n)
                eng.tensor_tensor(RFB[:, :, :], RF[g.h][:, :, :], B2R[:, :].unsqueeze(1).broadcast_to([P, GRAPHS, P]),
                                  ALU.mult).then_inc(pool_rfb, 1)

            def adj_eye(g):
                wait(eng, pe_tail, at(TAIL_PE, g.n - 2, "spread"))
                eng.tensor_tensor(AI[g.h][:, :, :], A[g.h][:, :, :], ident[:, :].unsqueeze(1).broadcast_to([P, GRAPHS, P]),
                                  ALU.add).then_inc(pool_ai, 1)

            def body(g, nxt, prev):
                def tail(stage):
                    if prev:
                        if stage == "base":
                            eng.wait_ge(s_XN, 16 * (prev.n + 1))
                        tail_pool(eng, prev.n, stage)

                if g:
                    rfb(g)
                tail("base")
                tail("dinv")
                if g:
                    adj_eye(g)
                if nxt:
                    squares(nxt)
                tail("rstd1")
                tail("scaled")
                tail("rstd2")

            eng.memset(ones[:, :], 1.0)
            eng.memset(halfc[:, :], 0.5)
            eng.memset(choose[:, :, :, :], 0.0).then_inc(s_pool, 1)
            eng.memset(minus_half[:, :], -0.5)
            eng.memset(ident[:, :], 0.0).then_inc(s_pool, 1)
            eng.memset(before[:, :], 1.0).then_inc(s_pool, 1)
            eng.iota(iota[:, :], [[1, P]], base=0, channel_multiplier=0, allow_small_or_imprecise_dtypes=True)
            eng.iota(POS, [[0, 1]], base=0, channel_multiplier=1, allow_small_or_imprecise_dtypes=True)
            eng.wait_ge(s_pool, 3)
            eng.affine_select(out=ident[:, :], in_=ident[:, :], compare_op=ALU.not_equal, fill=1.0,
                              base=0, pattern=[[-1, P]], channel_multiplier=1).then_inc(s_pool, 1)
            eng.affine_select(out=before[:, :], in_=before[:, :], compare_op=ALU.is_gt, fill=0.0,
                              base=0, pattern=[[1, P]], channel_multiplier=-1)
            for i in range(3):
                eng.wait_ge(s_pool, 3 + i + (i > 0))
                for q in range(GRAPHS):
                    last = eng.affine_select(out=choose[:, q, :, :].rearrange("r p (a k) -> r p a k", a=2),
                                             in_=choose[:, q, :, :].rearrange("r p (a k) -> r p a k", a=2),
                                             compare_op=ALU.not_equal, fill=1.0, base=-BLOCK * q - TOP * i,
                                             pattern=[[-2, PAIRS], [-1, 2], [0, NG]], channel_multiplier=1)
                last.then_inc(s_pool, 1)
            eng.wait_ge(s_pool, 7)
            eng.tensor_copy(identb[:, :], ident[:, :]).then_inc(s_setup, 1)
            eng.wait_ge(s_const, 16 * len(CONSTS))
            squares(Group(0, 0, 0))
            groups(eng, body)

            eng.wait_ge(s_verdict, 1)
            flagged = eng.value_load(verdict[0:1, 0:1])
            with eng.If(flagged != 0):
                with eng.Fori(0, dense_groups) as n:
                    eng.wait_ge(d_in, 48 * (n + 1))
                    eng.tensor_tensor(AI[0][:, :, :], A[0][:, :, :], ident[:, :].unsqueeze(1).broadcast_to([P, GRAPHS, P]),
                                      ALU.add).then_inc(dn_ai, 1)
                    for stage in ("base", "dinv", "rstd1", "scaled", "rstd2"):
                        tail_pool(eng, n + GROUPS, stage)


def kernel(**inputs):
    import concourse.bacc as bacc
    from concourse.bass_utils import run_bass_kernel_spmd

    def by_node(a):
        return np.ascontiguousarray(a).reshape(P, B * P)

    i = {k: np.asarray(v) for k, v in inputs.items()}
    column = lambda v: np.ascontiguousarray(v.reshape(P, 1))
    row = lambda v: np.ascontiguousarray(v.reshape(1, P))
    turned = lambda v: np.ascontiguousarray(v.T)
    offsets = -np.linspace(0.0, CUTOFF, NG, dtype=np.float32)
    arrays = {
        "adjT": by_node(i["adj"].transpose(2, 0, 1)),
        "x_nodes": by_node(i["x"].transpose(1, 0, 2)),
        "x_features": by_node(i["x"].transpose(2, 0, 1)),
        "w1T": turned(i["L0_gnn_W1"]), "b1": column(i["L0_gnn_b1"]),
        "w2T": turned(i["L0_gnn_W2"]), "b2": row(i["L0_gnn_b2"]),
        "waT": turned(i["L0_gnn_Wa"]),
        "wd1T": turned(i["L0_gnn_Wd1"]), "bd1": column(i["L0_gnn_bd1"]),
        "wd2T": turned(i["L0_gnn_Wd2"]), "bd2": row(i["L0_gnn_bd2"]),
        "wg": np.ascontiguousarray(i["L1_gnn_weight"]), "bg": row(i["L1_gnn_bias"]),
        "w1": np.ascontiguousarray(i["L0_gnn_W1"]),
        "offsets": column(np.concatenate([offsets, offsets])),
    }
    nc = bacc.Bacc("TRN2", target_bir_lowering=False, num_devices=1)
    args = [nc.dram_tensor(n, a.shape, mybir.dt.from_np(a.dtype), kind="ExternalInput").ap() for n, a in arrays.items()]
    out = nc.dram_tensor("out_nodes", (P, B * P), mybir.dt.float32, kind="ExternalOutput").ap()
    gnn_kernel(nc, *args, out)
    r = run_bass_kernel_spmd(nc, [arrays], core_ids=[0])
    return np.ascontiguousarray(r.results[0]["out_nodes"].reshape(P, B, P).transpose(1, 0, 2))
```

```python
import math
from collections import namedtuple
from contextlib import ExitStack

import numpy as np

import concourse.bass as bass
from concourse import mybir

B, P, NG = 64, 128, 64
CUTOFF = 5.0
LN2 = math.log(2.0)
EPS = 1e-5
GRAPHS = 4
GROUPS = B // GRAPHS
DIRECT = 4
LISTS = 2
SLOTS = DIRECT + LISTS
PAIRS = SLOTS // 2
TOP = 8
MORE = 2 * TOP
W = GRAPHS * P
BLOCK = P // GRAPHS
ROW = P + MORE + 1
PART = 2
SAFE = 30.0

PREP_DVE = ["top", "differ", "edge", "left", "more1", "left2", "more2", "differ2", "found", "lane",
            "count", "base", "end", "from", "pick", "place", "match", "value", "listed",
            "hi", "rest", "mid", "lo", "square"]
TAIL_PE = ["degree", "lin1", "lin2", "spread", "out"]
TAIL_DVE = ["degree", "soft", "sum1", "stats1", "moments1", "var1", "norm1",
            "sum2", "stats2", "moments2", "var2", "shift2"]
TAIL_ACT = ["abs", "exp", "log", "spread", "norm2"]
TAIL_POOL = ["base", "root", "power", "dinv", "rstd1", "scaled", "biased", "rstd2"]
DENSE = 4
DENSE_PAIRS = DENSE // 2
DENSE_PE = ["turn", "edge", "lin1", "lin2", "y"]
DENSE_DVE = ["hi", "rest", "mid", "lo", "clamp", "soft", "shift", "msg", "y"]
DENSE_ACT = ["turn", "square", "gauss", "exp", "log"]

WEIGHTS = 6 * P + NG + 3

Group = namedtuple("Group", "n half h")


def at(names, n, name):
    return n * len(names) + names.index(name) + 1


def wait(eng, sem, value):
    if not isinstance(value, int) or value > 0:
        eng.wait_ge(sem, value)


def gnn_kernel(nc, adjT, x, xT, weights, biases, out,
               force_dense=False, dense_groups=GROUPS):
    f32, bf16, i32 = mybir.dt.float32, mybir.dt.bfloat16, mybir.dt.int32
    ALU, ACT, AX = mybir.AluOpType, mybir.ActivationFunctionType, mybir.AxisListType
    width = np.linspace(0.0, CUTOFF, NG, dtype=np.float32)
    width = np.float32(width[1] - width[0])
    COEFF = float(np.float32(-0.5) / (width * width))

    with ExitStack() as ctx:
        def sb(name, shape, dt=f32):
            return ctx.enter_context(nc.sbuf_tensor(name, shape, dt))

        def pb(name):
            return ctx.enter_context(nc.psum_tensor(name, [P, W], f32))

        def sem(name):
            return ctx.enter_context(nc.semaphore(name))

        CW = sb("all_weights", [P, WEIGHTS])
        W1T, W2T, WAT, WD1T, WD2T, WG = (CW[:, bass.ts(i, P)] for i in range(6))
        W1 = CW[:, 6 * P:6 * P + NG]
        B1, BD1, NOFF = (CW[:, 6 * P + NG + i:6 * P + NG + i + 1] for i in range(3))
        CB = sb("all_biases", [P, 3 * P])
        B2R, BD2R, BGR = (CB[:, bass.ts(i, P)] for i in range(3))
        cols = sb("cols", [P, 4])
        B1L, BD1N, BOUND, B1ABS = (cols[:, i:i + 1] for i in range(4))
        BD2X = sb("BD2X", [P, P])
        ident, identb = sb("ident", [P, P]), sb("identb", [P, P], bf16)
        before, iota, place_of = sb("before", [P, P]), sb("iota", [P, LISTS * P]), sb("place_of", [P, LISTS])
        ones, minus_half = sb("ones", [P, 1]), sb("minus_half", [P, GRAPHS])
        w1abs = sb("w1abs", [P, NG])
        halfc = sb("halfc", [P, 1])

        A = [sb(f"A{h}", [P, GRAPHS, P]) for h in (0, 1)]
        XT = [sb(f"XT{h}", [P, GRAPHS, P]) for h in (0, 1)]
        XN = sb("XN", [P, GRAPHS, P])
        top = sb("top", [P, GRAPHS, TOP])
        differ = sb("differ", [P, GRAPHS, DIRECT])
        edge = [sb(f"edge{h}", [P, GRAPHS, SLOTS]) for h in (0, 1)]
        square = [sb(f"square{h}", [P, GRAPHS, SLOTS]) for h in (0, 1)]
        rest = sb("rest", [P, GRAPHS, SLOTS])
        packed = [sb(f"packed{h}", [P, GRAPHS, BLOCK], bf16) for h in (0, 1)]
        parts = [[packed[h][:, :, i * SLOTS:(i + 1) * SLOTS] for i in range(3)] for h in (0, 1)]
        turned = sb("turned", [P, P], bf16)
        chosen = sb("chosen", [P, GRAPHS, PAIRS, 2], bf16)
        choose = sb("choose", [P, GRAPHS * PAIRS * 2, NG], bf16)
        lane = sb("lane", [P, GRAPHS, ROW])
        more, left2 = sb("more", [P, GRAPHS, MORE]), sb("left2", [P, GRAPHS, P])
        differ2, found = sb("differ2", [P, GRAPHS, MORE]), sb("found", [P, GRAPHS, MORE])
        count, span_end = sb("count", [P, GRAPHS]), sb("span_end", [P, GRAPHS])
        started, pick = sb("started", [P, GRAPHS, LISTS * P]), sb("pick", [P, GRAPHS, LISTS * P])
        listed = [sb(f"listed{h}", [P, LISTS, GRAPHS, ROW]) for h in (0, 1)]
        place = sb("place", [P, LISTS, GRAPHS])
        match = sb("match", [P, LISTS * GRAPHS, MORE])
        flags = sb("flags", [P, 4, GRAPHS])
        least, unused = sb("least", [P, 1]), sb("unused", [P, GRAPHS, P])
        RF = [sb(f"RF{h}", [P, GRAPHS, 4, P]) for h in (0, 1)]
        RFB = sb("RFB", [P, GRAPHS, P])
        A2 = [sb(f"A2{h}", [P, GRAPHS, P]) for h in (0, 1)]
        AI = [sb(f"AI{h}", [P, GRAPHS, P]) for h in (0, 1)]
        hot = [sb(f"hot{h}", [P, SLOTS, P]) for h in (0, 1)]
        DIFF2, G = sb("DIFF2", [P, PAIRS, P]), sb("G", [P, PAIRS, P])
        EX = [sb(f"EX{i}", [P, PAIRS, P]) for i in (0, 1)]
        H = [sb(f"H{i}", [P, PAIRS, P]) for i in (0, 1)]
        Z = [sb(f"Z{i}", [P, PAIRS, P]) for i in (0, 1)]
        YS, UC, S1 = (sb(n, [P, GRAPHS, P]) for n in ("YS", "UC", "S1"))
        UE, UL, XB, R1, X1 = (sb(n, [P, GRAPHS, P]) for n in ("UE", "UL", "XB", "R1", "X1"))
        XS, X1B, SP, R2 = (sb(n, [P, GRAPHS, P]) for n in ("XS", "X1B", "SP", "R2"))
        OUT = sb("OUT", [P, GRAPHS, P])
        deg = sb("deg", [P, 5, GRAPHS])
        DEG0, DEG1, DEGN, ROOT, DINV = (deg[:, i, :] for i in range(5))
        stats = sb("stats", [P, GRAPHS, 6])
        mv = [sb(f"mv{i}", [P, GRAPHS, 2]) for i in (0, 1)]
        var = [sb(f"var{i}", [P, GRAPHS]) for i in (0, 1)]
        rstd = [sb(f"rstd{i}", [P, GRAPHS]) for i in (0, 1)]
        shift2 = sb("shift2", [P, GRAPHS])
        spare = sb("spare", [P, 1])
        worst, bad, verdict = sb("worst", [P, 1]), sb("bad", [P, 1]), sb("verdict", [1, 1], i32)
        VB, VR = sb("VB", [P, DENSE]), sb("VR", [P, DENSE])

        pE, pX0, pX1, pW0, pW1, pY, pM0, pM1 = (pb(n) for n in ("pE", "pX0", "pX1", "pW0", "pW1", "pY", "pM0", "pM1"))

        s_const, s_setup = sem("consts_loaded"), sem("consts_made")
        s_A = [sem(f"adj_loaded{h}") for h in (0, 1)]
        s_XT = [sem(f"xT_loaded{h}") for h in (0, 1)]
        s_XN, s_out = sem("x_loaded"), sem("out_stored")
        pe_e, pe_x = sem("edges_spread"), [sem(f"lin1_done{i}") for i in (0, 1)]
        pe_share, s_bd2x = sem("b2_share_done"), sem("second_bias_done")
        pe_w, pe_s = [sem(f"filter_done{i}") for i in (0, 1)], [sem(f"summed{i}") for i in (0, 1)]
        act_e, act_g = sem("diff_squared"), sem("gauss_done")
        act_x, act_h = [sem(f"exp_done{i}") for i in (0, 1)], [sem(f"soft_done{i}") for i in (0, 1)]
        dve_hot, dve_z = sem("hot_done"), [sem(f"message_done{i}") for i in (0, 1)]
        dve_prep = sem("prep_dve")
        pe_rf, act_rf, pe_base = sem("rf_done"), sem("rf_copied"), sem("starts_done")
        pe_look, act_look = sem("looked_up"), sem("listed_copied")
        pe_turn, act_turned = sem("parts_turned"), sem("turned_copied")
        pe_lrf, act_lrf = sem("list_rf_done"), sem("list_rf_copied")
        pool_sq, pool_rfb, pool_ai = sem("squares_done"), sem("rfb_done"), sem("adj_eye_done")
        act_least, dve_least = sem("negatives_summed"), sem("negatives_noted")
        act_y = sem("y_copied")
        pe_tail, dve_tail, act_tail, pool_tail = sem("tail_pe"), sem("tail_dve"), sem("tail_act"), sem("tail_pool")
        s_verdict, s_count, s_bound, s_pool = sem("verdict"), sem("bad_counted"), sem("bound_done"), sem("pool_consts")
        d_in, d_block, d_store = sem("dense_in"), sem("dense_block"), sem("dense_stored")
        dn_pe, dn_dve, dn_act = sem("dense_pe"), sem("dense_dve"), sem("dense_act")
        dn_rf, dn_rfc, dn_ai, dn_free = sem("dense_rf"), sem("dense_rf_copied"), sem("dense_adj_eye"), sem("dense_block_free")

        block = ctx.enter_context(nc.Block())

        def groups(eng, body):
            def step(n, half, h):
                first, left = isinstance(n, int) and n == 0, GROUPS - 1 - n if isinstance(n, int) else GROUPS
                body(Group(n, half, h), Group(n + 1, half + h, 1 - h) if left > 0 else None,
                     None if first else Group(n - 1, half - 1 + h, 1 - h),
                     Group(n + 2, half + 1, h) if left > 1 else None,
                     n - 2 if not isinstance(n, int) or n > 1 else None)

            step(0, 0, 0)
            step(1, 0, 1)
            with eng.Fori(0, GROUPS // 2 - 2) as t:
                step(2 * t + 2, t + 1, 0)
                step(2 * t + 3, t + 1, 1)
            step(GROUPS - 2, GROUPS // 2 - 1, 0)
            step(GROUPS - 1, GROUPS // 2 - 1, 1)
            body(None, None, Group(GROUPS - 1, GROUPS // 2 - 1, 1), None, GROUPS - 2)

        @block.sync
        def _(eng):
            def store(c):
                eng.wait_ge(act_tail, at(TAIL_ACT, c, "norm2"))
                eng.dma_start(out[:, bass.ds(c * W, W)], OUT[:, :, :]).then_inc(s_out, 16)

            def load_adj(g, n):
                eng.dma_start(A[g.h][:, :, :], adjT[:, bass.ds(n * W, W)]).then_inc(s_A[g.h], 16)

            def load_xT(g, n):
                eng.dma_start(XT[g.h][:, :, :], xT[:, bass.ds(n * W, W)]).then_inc(s_XT[g.h], 16)

            def body(g, nxt, prev, later, ended):
                if g:
                    n = g.n
                    if later:
                        wait(eng, pe_rf, n + 1)
                        load_xT(g, n + 2)
                    if prev:
                        wait(eng, pool_tail, at(TAIL_POOL, n - 1, "base"))
                    eng.dma_start(XN[:, :, :], x[:, bass.ds(n * W, W)]).then_inc(s_XN, 16)
                if ended is not None:
                    store(ended)
                if later:
                    eng.wait_ge(dve_hot, GRAPHS * (n + 1))
                    eng.wait_ge(pool_ai, n + 1)
                    eng.wait_ge(act_least, n + 1)
                    load_adj(g, n + 2)
                if not g:
                    store(prev.n)

            eng.sem_inc(s_out, 16)
            load_adj(Group(0, 0, 0), 0)
            load_xT(Group(0, 0, 0), 0)
            eng.dma_start(CW[:, :], weights).then_inc(s_const, 16)
            eng.dma_start(CB[:, :], biases.broadcast_to([P, 3 * P])).then_inc(s_const, 16)
            load_adj(Group(1, 0, 1), 1)
            load_xT(Group(1, 0, 1), 1)
            groups(eng, body)
            eng.wait_ge(s_out, 16 * (GROUPS + 1))

            eng.wait_ge(s_verdict, 1)
            flagged = eng.value_load(verdict[0:1, 0:1])
            with eng.If(flagged != 0):
                with eng.Fori(0, dense_groups) as n:
                    eng.dma_start(A[0][:, :, :], adjT[:, bass.ds(n * W, W)]).then_inc(d_in, 16)
                    eng.dma_start(XT[0][:, :, :], xT[:, bass.ds(n * W, W)]).then_inc(d_in, 16)
                    eng.dma_start(XN[:, :, :], x[:, bass.ds(n * W, W)]).then_inc(d_in, 16)
                    with eng.Fori(0, GRAPHS) as q:
                        with eng.Fori(0, P // DENSE) as t:
                            k = (n * GRAPHS + q) * (P // DENSE) + t
                            eng.dma_start(VB[:, :], adjT[:, bass.ds(n * W + q * P + t * DENSE, DENSE)]).then_inc(d_block, 16)
                            eng.wait_ge(dn_dve, (k + 1) * len(DENSE_DVE))
                            eng.sem_inc(dn_free, 1)
                    eng.wait_ge(act_tail, at(TAIL_ACT, n + GROUPS, "norm2"))
                    eng.dma_start(out[:, bass.ds(n * W, W)], OUT[:, :, :]).then_inc(d_store, 16)
                    eng.wait_ge(d_store, 16 * (n + 1))
                    eng.sem_inc(dn_free, 1)

        def tail_pe(eng, c, n, h, stage):
            if stage == "degree":
                if h is None:
                    eng.wait_ge(dn_ai, c - GROUPS + 1)
                else:
                    eng.wait_ge(pool_ai, c + 1)
                wait(eng, dve_tail, at(TAIL_DVE, c - 1, "sum2"))
                for q in range(GRAPHS):
                    last = eng.matmul(pM0[:, q:q + 1], AI[h or 0][:, q, :], ones[:, :], start=True, stop=True)
                last.then_inc(pe_tail, 1)
            if stage == "lin1":
                eng.wait_ge(act_y, c + 1)
                eng.wait_ge(dve_tail, at(TAIL_DVE, c, "degree"))
                eng.matmul(pM0[:, :], WD1T, YS[:, :, :], start=True, stop=True).then_inc(pe_tail, 1)
            if stage == "lin2":
                eng.wait_ge(dve_tail, at(TAIL_DVE, c, "soft"))
                for q in range(GRAPHS):
                    last = eng.matmul(pM0[:, bass.ts(q, P)], S1[:, q, :], WD2T, start=True, stop=True)
                last.then_inc(pe_tail, 1)
            if stage == "spread":
                eng.wait_ge(pool_tail, at(TAIL_POOL, c, "scaled"))
                for q in range(GRAPHS):
                    last = eng.matmul(pM0[:, bass.ts(q, P)], XS[:, q, :], AI[h or 0][:, q, :], start=True, stop=True)
                last.then_inc(pe_tail, 1)
            if stage == "out":
                eng.wait_ge(act_tail, at(TAIL_ACT, c, "spread"))
                for q in range(GRAPHS):
                    last = eng.matmul(pM0[:, bass.ts(q, P)], SP[:, q, :], WG, start=True, stop=True)
                last.then_inc(pe_tail, 1)

        def tail_act(eng, c, stage):
            if stage == "soft":
                eng.wait_ge(pe_tail, at(TAIL_PE, c, "lin1"))
                eng.activation(UC[:, :, :], pM0[:, :], ACT.Abs, bias=BD1).then_inc(act_tail, 1)
                eng.wait_ge(act_tail, at(TAIL_ACT, c, "abs"))
                eng.activation(UE[:, :, :], UC[:, :, :], ACT.Exp, scale=-1.0).then_inc(act_tail, 1)
                eng.wait_ge(act_tail, at(TAIL_ACT, c, "exp"))
                wait(eng, dve_tail, at(TAIL_DVE, c - 1, "soft"))
                eng.activation(UL[:, :, :], UE[:, :, :], ACT.Ln, bias=halfc[:, :], scale=0.5).then_inc(act_tail, 1)
            if stage == "spread":
                eng.wait_ge(pe_tail, at(TAIL_PE, c, "spread"))
                eng.activation(SP[:, :, :], pM0[:, :], ACT.Copy).then_inc(act_tail, 1)
            if stage == "norm2":
                eng.wait_ge(dve_tail, at(TAIL_DVE, c, "shift2"))
                for q in range(GRAPHS):
                    last = eng.activation(OUT[:, q, :], R2[:, q, :], ACT.Identity, bias=shift2[:, q:q + 1],
                                          scale=rstd[1][:, q:q + 1])
                last.then_inc(act_tail, 1)

        def layer_norm_stats(eng, c, i, R):
            eng.wait_ge(dve_tail, at(TAIL_DVE, c, f"sum{i + 1}"))
            for q in range(GRAPHS):
                last = eng.bn_stats(stats[:, q, :], R[:, q, :])
            last.then_inc(dve_tail, 1)
            eng.wait_ge(dve_tail, at(TAIL_DVE, c, f"stats{i + 1}"))
            eng.memset(spare[:, :], 0.0)
            for q in range(GRAPHS):
                last = eng.bn_aggr(mv[i][:, q, :], stats[:, q, :])
            last.then_inc(dve_tail, 1)
            eng.wait_ge(dve_tail, at(TAIL_DVE, c, f"moments{i + 1}"))
            eng.tensor_scalar(var[i][:, :], mv[i][:, :, 1], EPS, None, ALU.add).then_inc(dve_tail, 1)

        def tail_dve(eng, c, stage):
            if stage == "degree":
                eng.wait_ge(pe_tail, at(TAIL_PE, c, "degree"))
                wait(eng, pool_tail, at(TAIL_POOL, c - 1, "biased"))
                eng.tensor_scalar(DEG0, pM0[:, 0:GRAPHS], 0.0, None, ALU.is_equal)
                eng.tensor_scalar(DEGN, pM0[:, 0:GRAPHS], 0.0, None, ALU.not_equal)
                eng.tensor_copy(DEG1, pM0[:, 0:GRAPHS]).then_inc(dve_tail, 1)
            if stage == "soft":
                eng.wait_ge(act_tail, at(TAIL_ACT, c, "log"))
                eng.scalar_tensor_tensor(S1[:, :, :], pM0[:, :], BD1N, UL[:, :, :], ALU.max, ALU.add).then_inc(dve_tail, 1)
            if stage == "sum1":
                eng.wait_ge(pe_tail, at(TAIL_PE, c, "lin2"))
                eng.wait_ge(pool_tail, at(TAIL_POOL, c, "base"))
                eng.tensor_tensor(R1[:, :, :], pM0[:, :], XB[:, :, :], ALU.add).then_inc(dve_tail, 1)
                layer_norm_stats(eng, c, 0, R1)
            if stage == "norm1":
                eng.wait_ge(pool_tail, at(TAIL_POOL, c, "rstd1"))
                for q in range(GRAPHS):
                    last = eng.tensor_scalar(X1[:, q, :], R1[:, q, :], mv[0][:, q, 0:1], rstd[0][:, q:q + 1],
                                             ALU.subtract, ALU.mult)
                last.then_inc(dve_tail, 1)
            if stage == "sum2":
                eng.wait_ge(pe_tail, at(TAIL_PE, c, "out"))
                wait(eng, act_tail, at(TAIL_ACT, c - 1, "norm2"))
                eng.wait_ge(pool_tail, at(TAIL_POOL, c, "biased"))
                for q in range(GRAPHS):
                    last = eng.scalar_tensor_tensor(R2[:, q, :], pM0[:, bass.ts(q, P)], DINV[:, q:q + 1],
                                                    X1B[:, q, :], ALU.mult, ALU.add)
                last.then_inc(dve_tail, 1)
                layer_norm_stats(eng, c, 1, R2)
            if stage == "shift2":
                eng.wait_ge(pool_tail, at(TAIL_POOL, c, "rstd2"))
                eng.scalar_tensor_tensor(shift2[:, :], mv[1][:, :, 0], -1.0, rstd[1][:, :], ALU.mult, ALU.mult)\
                   .then_inc(dve_tail, 1)

        def tail_pool(eng, c, stage):
            if stage == "base":
                wait(eng, dve_tail, at(TAIL_DVE, c - 1, "sum1"))
                eng.tensor_tensor(XB[:, :, :], XN[:, :, :], BD2X[:, :].unsqueeze(1).broadcast_to([P, GRAPHS, P]),
                                  ALU.add).then_inc(pool_tail, 1)
            if stage == "dinv":
                eng.wait_ge(dve_tail, at(TAIL_DVE, c, "degree"))
                eng.tensor_tensor(ROOT, DEG1, DEG0, ALU.add).then_inc(pool_tail, 1)
                eng.wait_ge(pool_tail, at(TAIL_POOL, c, "root"))
                eng.tensor_tensor(ROOT, ROOT, minus_half[:, :], ALU.pow).then_inc(pool_tail, 1)
                eng.wait_ge(pool_tail, at(TAIL_POOL, c, "power"))
                eng.tensor_tensor(DINV, ROOT, DEGN, ALU.mult).then_inc(pool_tail, 1)
            if stage in ("rstd1", "rstd2"):
                i = int(stage[-1]) - 1
                eng.wait_ge(dve_tail, at(TAIL_DVE, c, f"var{i + 1}"))
                eng.tensor_tensor(rstd[i][:, :], var[i][:, :], minus_half[:, :], ALU.pow).then_inc(pool_tail, 1)
            if stage == "scaled":
                eng.wait_ge(dve_tail, at(TAIL_DVE, c, "norm1"))
                eng.tensor_tensor(XS[:, :, :], X1[:, :, :], DINV.unsqueeze(2).broadcast_to([P, GRAPHS, P]),
                                  ALU.mult).then_inc(pool_tail, 1)
                eng.tensor_tensor(X1B[:, :, :], X1[:, :, :], BGR.unsqueeze(1).broadcast_to([P, GRAPHS, P]),
                                  ALU.add).then_inc(pool_tail, 1)

        def spread_edges(eng, q, pairs=PAIRS):
            for p in range(pairs):
                k = (q * PAIRS + p) * 2
                last = eng.matmul(pE[:, bass.ts(p, P)], choose[:, k:k + 2, :], turned[:, :], start=True, stop=True)
            return last

        @block.tensor
        def _(eng):
            def project(g):
                eng.wait_ge(s_XT[g.h], 16 * (g.half + 1))
                wait(eng, act_lrf, LISTS * g.n)
                for q in range(GRAPHS):
                    last = eng.matmul(pM1[:, bass.ts(q, P)], XT[g.h][:, q, :], WAT, start=True, stop=True)
                last.then_inc(pe_rf, 1)

            def starts(g):
                eng.wait_ge(dve_prep, at(PREP_DVE, g.n, "count"))
                eng.wait_ge(act_rf, g.n + 1)
                eng.matmul(pM1[:, 0:GRAPHS], before[:, :], count[:, :], start=True, stop=True).then_inc(pe_base, 1)

            def look_up(g, k):
                if k == 0:
                    eng.wait_ge(dve_prep, at(PREP_DVE, g.n, "pick"))
                wait(eng, act_look, 4 * g.n + k)
                for j in range(PART):
                    q = PART * (k % 2) + j
                    last = eng.matmul(pM1[:, bass.ts(j, ROW)], pick[:, q, bass.ts(k // 2, P)], lane[:, q, :],
                                      start=True, stop=True)
                last.then_inc(pe_look, 1)

            def turn(g):
                eng.wait_ge(dve_prep, at(PREP_DVE, g.n, "lo"))
                eng.matmul(pM1[:, 0:P], packed[g.h][:, :, :], identb[:, :], start=True, stop=True).then_inc(pe_turn, 1)

            def list_rf(g, l):
                eng.wait_ge(act_turned, g.n + 1)
                wait(eng, act_lrf, LISTS * g.n + l)
                for q in range(GRAPHS):
                    last = eng.matmul(pM1[:, bass.ts(q, P)], pick[:, q, bass.ts(l, P)], RF[g.h][:, q, 1, :],
                                      start=True, stop=True)
                last.then_inc(pe_lrf, 1)

            def spread(g, q):
                u = GRAPHS * g.n + q
                if q == 0:
                    eng.wait_ge(act_turned, g.n + 1)
                wait(eng, act_e, u)
                spread_edges(eng, q).then_inc(pe_e, 1)

            def lin1(g, q):
                u = GRAPHS * g.n + q
                eng.wait_ge(act_g, u + 1)
                wait(eng, act_x[0], u)
                wait(eng, act_x[1], u)
                eng.matmul(pX0[:, 0:PAIRS * P], W1T[0:NG, :], G[0:NG, :, :], start=True, stop=True).then_inc(pe_x[0], 1)
                eng.matmul(pX1[:, 0:PAIRS * P], W1T[NG:P, :], G[NG:P, :, :], start=True, stop=True).then_inc(pe_x[1], 1)

            def lin2(g, q, i):
                u = GRAPHS * g.n + q
                eng.wait_ge(act_h[i], u + 1)
                wait(eng, dve_z[i], u)
                for p in range(PAIRS):
                    last = eng.matmul((pW0, pW1)[i][:, bass.ts(p, P)], H[i][:, p, :], W2T, start=True, stop=True)
                last.then_inc(pe_w[i], 1)

            def shared(g, q):
                if q == 0:
                    eng.wait_ge(pool_rfb, g.n + 1)
                    eng.wait_ge(pool_sq, g.n + 1)
                    wait(eng, act_y, g.n)
                eng.matmul(pY[:, bass.ts(q, P)], RFB[:, q, :], A2[g.h][:, q, :], start=q == 0, stop=False,
                           skip_group_check=True).then_inc(pe_share, 1)

            def messages(g, q, i):
                u = GRAPHS * g.n + q
                if i == 0:
                    eng.wait_ge(dve_hot, u + 1)
                eng.wait_ge(dve_z[i], u + 1)
                for p in range(PAIRS):
                    last = eng.matmul(pY[:, bass.ts(q, P)], Z[i][:, p, :], hot[q % 2][:, 2 * p + i, :],
                                      start=False, stop=False, skip_group_check=True)
                last.then_inc(pe_s[i], 1)

            def body(g, nxt, prev, later, ended):
                def tail(stage):
                    if prev:
                        tail_pe(eng, prev.n, prev.n, prev.h, stage)

                if not g:
                    for stage in TAIL_PE:
                        tail(stage)
                    return
                lin2(g, 0, 0)
                lin2(g, 0, 1)
                if nxt:
                    project(nxt)
                lin1(g, 1)
                spread(g, 2)
                tail("degree")
                shared(g, 0)
                messages(g, 0, 0)
                messages(g, 0, 1)
                tail("lin1")

                lin2(g, 1, 0)
                if nxt:
                    starts(nxt)
                lin1(g, 2)
                spread(g, 3)
                lin2(g, 1, 1)
                tail("lin2")
                shared(g, 1)
                messages(g, 1, 0)
                if nxt:
                    look_up(nxt, 0)
                messages(g, 1, 1)
                if nxt:
                    look_up(nxt, 1)

                lin2(g, 2, 0)
                lin1(g, 3)
                if nxt:
                    look_up(nxt, 2)
                lin2(g, 2, 1)
                shared(g, 2)
                messages(g, 2, 0)
                if nxt:
                    look_up(nxt, 3)
                messages(g, 2, 1)

                lin2(g, 3, 0)
                lin2(g, 3, 1)
                tail("spread")
                shared(g, 3)
                if nxt:
                    turn(nxt)
                messages(g, 3, 0)
                if nxt:
                    spread(nxt, 0)
                if nxt:
                    list_rf(nxt, 0)
                messages(g, 3, 1)
                tail("out")
                if nxt:
                    lin1(nxt, 0)
                    list_rf(nxt, 1)
                    spread(nxt, 1)

            eng.wait_ge(s_const, 32)
            eng.wait_ge(s_setup, 2)
            eng.matmul(pM0[:, 0:P], BD1.broadcast_to([P, P]), WD2T, start=True, stop=True).then_inc(s_count, 1)
            first = Group(0, 0, 0)
            project(first)
            starts(first)
            for k in range(4):
                look_up(first, k)
            turn(first)
            spread(first, 0)
            list_rf(first, 0)
            lin1(first, 0)
            list_rf(first, 1)
            spread(first, 1)
            groups(eng, body)

            eng.wait_ge(s_count, 2)
            eng.matmul(pM1[0:1, 0:1], bad[:, :], ones[:, :], start=True, stop=True).then_inc(s_count, 1)
            eng.wait_ge(s_verdict, 1)
            flagged = eng.value_load(verdict[0:1, 0:1])
            with eng.If(flagged != 0):
                with eng.Fori(0, dense_groups) as n:
                    eng.wait_ge(d_in, 48 * (n + 1))
                    for q in range(GRAPHS):
                        last = eng.matmul(pM1[:, bass.ts(q, P)], XT[0][:, q, :], WAT, start=True, stop=True)
                    last.then_inc(dn_rf, 1)
                    with eng.Fori(0, GRAPHS * P // DENSE) as m:
                        k = n * (GRAPHS * P // DENSE) + m
                        eng.wait_ge(dn_dve, at(DENSE_DVE, k, "lo"))
                        eng.matmul(pW0[:, 0:P], packed[0][:, :, :], identb[:, :], start=True, stop=True).then_inc(dn_pe, 1)
                        eng.wait_ge(dn_act, at(DENSE_ACT, k, "turn"))
                        spread_edges(eng, 0, DENSE_PAIRS).then_inc(dn_pe, 1)
                        eng.wait_ge(dn_act, at(DENSE_ACT, k, "gauss"))
                        width = DENSE_PAIRS * P
                        eng.matmul(pX0[:, 0:width], W1T[0:NG, :], G[0:NG, 0:DENSE_PAIRS, :], start=True, stop=True)
                        eng.matmul(pX1[:, 0:width], W1T[NG:P, :], G[NG:P, 0:DENSE_PAIRS, :], start=True, stop=True)\
                           .then_inc(dn_pe, 1)
                        eng.wait_ge(dn_dve, at(DENSE_DVE, k, "soft"))
                        for i in (0, 1):
                            for p in range(DENSE_PAIRS):
                                last = eng.matmul((pW0, pW1)[i][:, bass.ts(p, P)], H[i][:, p, :], W2T,
                                                  start=True, stop=True)
                        last.then_inc(dn_pe, 1)
                        eng.wait_ge(dn_dve, at(DENSE_DVE, k, "msg"))
                        for s in range(DENSE):
                            last = eng.matmul(pY[:, s:s + 1], Z[s % 2][:, s // 2, :], square[0][:, 0, s:s + 1],
                                              start=True, stop=True)
                        last.then_inc(dn_pe, 1)
                    for stage in TAIL_PE:
                        tail_pe(eng, n + GROUPS, n, None, stage)

        @block.scalar
        def _(eng):
            def squares(g, q):
                u = GRAPHS * g.n + q
                eng.wait_ge(pe_e, u + 1)
                eng.activation(DIFF2[:, :, :], pE[:, 0:PAIRS * P], ACT.Square, bias=NOFF).then_inc(act_e, 1)
                eng.wait_ge(act_e, u + 1)
                wait(eng, pe_x[1], u)
                eng.activation(G[:, :, :], DIFF2[:, :, :], ACT.Exp, scale=COEFF).then_inc(act_g, 1)

            def soft(g, q, i):
                u = GRAPHS * g.n + q
                eng.wait_ge(pe_x[i], u + 1)
                eng.activation(EX[i][:, :, :], (pX0, pX1)[i][:, 0:PAIRS * P], ACT.Exp, bias=B1).then_inc(act_x[i], 1)
                eng.wait_ge(act_x[i], u + 1)
                wait(eng, pe_w[i], u)
                eng.activation(H[i][:, :, :], EX[i][:, :, :], ACT.Ln, bias=halfc[:, :], scale=0.5).then_inc(act_h[i], 1)

            def copy_rf(g):
                eng.wait_ge(pe_rf, g.n + 1)
                wait(eng, dve_z[1], GRAPHS * (g.n - 1))
                wait(eng, pool_rfb, g.n - 1)
                rf = pM1[:, :].rearrange("p (a b) -> p a b", b=P)
                eng.activation(RF[g.h][:, :, 1, :], rf, ACT.Copy)
                eng.activation(RF[g.h][:, :, 2, :], rf, ACT.Copy).then_inc(act_rf, 1)

            def copy_list_rf(g, l):
                eng.wait_ge(pe_lrf, LISTS * g.n + l + 1)
                eng.activation(RF[g.h][:, :, 3 * l, :], pM1[:, :].rearrange("p (a b) -> p a b", b=P), ACT.Copy)\
                   .then_inc(act_lrf, 1)

            def copy_listed(g, k):
                eng.wait_ge(pe_look, 4 * g.n + k + 1)
                wait(eng, dve_hot, GRAPHS * (g.n - 1))
                q = PART * (k % 2)
                eng.activation(listed[g.h][:, k // 2, q:q + PART, :],
                               pM1[:, 0:PART * ROW].rearrange("p (a b) -> p a b", b=ROW), ACT.Copy).then_inc(act_look, 1)

            def copy_turned(g):
                eng.wait_ge(pe_turn, g.n + 1)
                eng.activation(turned[:, :], pM1[:, 0:P], ACT.Copy).then_inc(act_turned, 1)

            def copy_y(g):
                eng.wait_ge(pe_s[1], GRAPHS * (g.n + 1))
                wait(eng, pe_tail, at(TAIL_PE, g.n - 1, "lin1"))
                eng.activation(YS[:, :, :], pY[:, :], ACT.Copy).then_inc(act_y, 1)

            def negatives(g):
                eng.wait_ge(s_A[g.h], 16 * (g.half + 1))
                wait(eng, dve_least, g.n)
                eng.activation(unused[:, :, :], A[g.h][:, :, :], ACT.Relu, scale=-1.0, accum_out=least[:, :])\
                   .then_inc(act_least, 1)

            def body(g, nxt, prev, later, ended):
                def norm2(c):
                    eng.wait_ge(s_out, 16 * (c + 1))
                    tail_act(eng, c, "norm2")

                if not g:
                    copy_y(prev)
                    norm2(ended)
                    for stage in ("soft", "spread"):
                        tail_act(eng, prev.n, stage)
                    norm2(prev.n)
                    return
                if prev:
                    copy_y(prev)
                if nxt:
                    copy_rf(nxt)
                soft(g, 1, 0)
                soft(g, 1, 1)
                squares(g, 2)
                if ended is not None:
                    norm2(ended)
                if prev:
                    tail_act(eng, prev.n, "soft")

                soft(g, 2, 0)
                soft(g, 2, 1)
                squares(g, 3)
                negatives(g)
                if nxt:
                    copy_listed(nxt, 0)
                    copy_listed(nxt, 1)

                soft(g, 3, 0)
                if nxt:
                    copy_listed(nxt, 2)
                soft(g, 3, 1)
                if nxt:
                    copy_listed(nxt, 3)

                if prev:
                    tail_act(eng, prev.n, "spread")
                if nxt:
                    copy_turned(nxt)
                    squares(nxt, 0)
                    copy_list_rf(nxt, 0)
                    soft(nxt, 0, 0)
                    soft(nxt, 0, 1)
                    copy_list_rf(nxt, 1)
                    squares(nxt, 1)

            eng.preload_act_table_set("natural_log_exp_and_others")
            eng.wait_ge(s_const, 32)
            eng.wait_ge(s_setup, 2)
            first = Group(0, 0, 0)
            copy_rf(first)
            for k in range(4):
                copy_listed(first, k)
            copy_turned(first)
            squares(first, 0)
            copy_list_rf(first, 0)
            soft(first, 0, 0)
            soft(first, 0, 1)
            copy_list_rf(first, 1)
            squares(first, 1)
            groups(eng, body)

            eng.wait_ge(s_verdict, 1)
            flagged = eng.value_load(verdict[0:1, 0:1])
            with eng.If(flagged != 0):
                with eng.Fori(0, dense_groups) as n:
                    eng.wait_ge(dn_rf, n + 1)
                    eng.activation(RF[0][:, :, 1, :], pM1[:, :].rearrange("p (a b) -> p a b", b=P), ACT.Copy)\
                       .then_inc(dn_rfc, 1)
                    with eng.Fori(0, GRAPHS * P // DENSE) as m:
                        k = n * (GRAPHS * P // DENSE) + m
                        eng.wait_ge(dn_pe, at(DENSE_PE, k, "turn"))
                        eng.activation(turned[:, :], pW0[:, 0:P], ACT.Copy).then_inc(dn_act, 1)
                        eng.wait_ge(dn_pe, at(DENSE_PE, k, "edge"))
                        some = slice(0, DENSE_PAIRS)
                        eng.activation(DIFF2[:, some, :], pE[:, 0:DENSE_PAIRS * P], ACT.Square, bias=NOFF)\
                           .then_inc(dn_act, 1)
                        eng.wait_ge(dn_act, at(DENSE_ACT, k, "square"))
                        eng.activation(G[:, some, :], DIFF2[:, some, :], ACT.Exp, scale=COEFF).then_inc(dn_act, 1)
                        eng.wait_ge(dn_dve, at(DENSE_DVE, k, "clamp"))
                        for i in (0, 1):
                            last = eng.activation(H[i][:, some, :], EX[i][:, some, :], ACT.Exp)
                        last.then_inc(dn_act, 1)
                        eng.wait_ge(dn_act, at(DENSE_ACT, k, "exp"))
                        for i in (0, 1):
                            last = eng.activation(EX[i][:, some, :], H[i][:, some, :], ACT.Ln, bias=halfc[:, :], scale=0.5)
                        last.then_inc(dn_act, 1)
                    for stage in ("soft", "spread", "norm2"):
                        tail_act(eng, n + GROUPS, stage)

        @block.vector
        def _(eng):
            def parts_of(value, exact, left_over, sem_, names, k):
                eng.tensor_copy(exact[0], value).then_inc(sem_, 1)
                eng.wait_ge(sem_, at(names, k, "hi"))
                eng.tensor_tensor(left_over, value, exact[0], ALU.subtract).then_inc(sem_, 1)
                eng.wait_ge(sem_, at(names, k, "rest"))
                eng.tensor_copy(exact[1], left_over).then_inc(sem_, 1)
                eng.wait_ge(sem_, at(names, k, "mid"))
                eng.tensor_tensor(exact[2], left_over, exact[1], ALU.subtract).then_inc(sem_, 1)

            def prep_top(g):
                n, h = g.n, g.h
                eng.wait_ge(s_A[h], 16 * (g.half + 1))
                eng.memset(spare[:, :], 0.0)
                for q in range(GRAPHS):
                    last = eng.max(top[:, q, :], A[h][:, q, :])
                last.then_inc(dve_prep, 1)
                eng.wait_ge(dve_prep, at(PREP_DVE, n, "top"))
                eng.tensor_tensor(differ[:, :, 1:DIRECT], top[:, :, 1:DIRECT], top[:, :, 0:DIRECT - 1],
                                  ALU.not_equal).then_inc(dve_prep, 1)
                eng.wait_ge(dve_prep, at(PREP_DVE, n, "differ"))
                eng.tensor_copy(edge[h][:, :, 1:2], top[:, :, 0:1])
                eng.tensor_tensor(edge[h][:, :, 2:1 + DIRECT], top[:, :, 1:DIRECT], differ[:, :, 1:DIRECT],
                                  ALU.mult).then_inc(dve_prep, 1)

            def prep_left(g):
                n, h = g.n, g.h
                wait(eng, pe_look, 4 * n)
                for q in range(GRAPHS):
                    last = eng.scalar_tensor_tensor(lane[:, q, 0:P], A[h][:, q, :], top[:, q, DIRECT - 1:DIRECT],
                                                    A[h][:, q, :], ALU.is_lt, ALU.mult)
                last.then_inc(dve_prep, 1)
                eng.wait_ge(dve_prep, at(PREP_DVE, n, "left"))
                eng.memset(spare[:, :], 0.0)
                for q in range(GRAPHS):
                    last = eng.max(more[:, q, 0:TOP], lane[:, q, 0:P])
                last.then_inc(dve_prep, 1)

            def prep_more(g):
                n, h = g.n, g.h
                eng.wait_ge(dve_prep, at(PREP_DVE, n, "more1"))
                for q in range(GRAPHS):
                    last = eng.scalar_tensor_tensor(left2[:, q, :], lane[:, q, 0:P], more[:, q, TOP - 1:TOP],
                                                    lane[:, q, 0:P], ALU.is_lt, ALU.mult)
                last.then_inc(dve_prep, 1)
                eng.wait_ge(dve_prep, at(PREP_DVE, n, "left2"))
                eng.memset(spare[:, :], 0.0)
                for q in range(GRAPHS):
                    last = eng.max(more[:, q, TOP:MORE], left2[:, q, :])
                last.then_inc(dve_prep, 1)
                eng.wait_ge(dve_prep, at(PREP_DVE, n, "more2"))
                eng.tensor_tensor(differ2[:, :, 1:MORE], more[:, :, 1:MORE], more[:, :, 0:MORE - 1],
                                  ALU.not_equal).then_inc(dve_prep, 1)
                eng.tensor_scalar(found[:, :, :], more[:, :, :], 0.0, None, ALU.is_gt).then_inc(dve_prep, 1)
                eng.tensor_tensor(flags[:, 0, :], flags[:, 0, :], more[:, :, MORE - 1], ALU.max)
                eng.wait_ge(dve_prep, at(PREP_DVE, n, "found"))
                eng.tensor_copy(lane[:, :, P:P + 1], more[:, :, 0:1])
                eng.tensor_tensor(lane[:, :, P + 1:P + MORE], more[:, :, 1:MORE], differ2[:, :, 1:MORE],
                                  ALU.mult).then_inc(dve_prep, 1)
                eng.reduce_sum(count[:, :], found[:, :, :], AX.X).then_inc(dve_prep, 1)

            def prep_pick(g):
                n = g.n
                eng.wait_ge(pe_base, n + 1)
                eng.tensor_copy(lane[:, :, P + MORE], pM1[:, 0:GRAPHS]).then_inc(dve_prep, 1)
                eng.tensor_tensor(span_end[:, :], pM1[:, 0:GRAPHS], count[:, :], ALU.add).then_inc(dve_prep, 1)
                eng.wait_ge(dve_prep, at(PREP_DVE, n, "end"))
                for q in range(GRAPHS):
                    last = eng.tensor_scalar(started[:, q, :], iota[:, :], lane[:, q, P + MORE:ROW], None, ALU.is_ge)
                last.then_inc(dve_prep, 1)
                eng.scalar_tensor_tensor(flags[:, 1, :], span_end[:, :], float(LISTS * P), flags[:, 1, :],
                                         ALU.subtract, ALU.max)
                eng.wait_ge(dve_prep, at(PREP_DVE, n, "from"))
                wait(eng, pe_lrf, LISTS * n)
                for q in range(GRAPHS):
                    last = eng.scalar_tensor_tensor(pick[:, q, :], iota[:, :], span_end[:, q:q + 1], started[:, q, :],
                                                    ALU.is_lt, ALU.mult)
                last.then_inc(dve_prep, 1)

            def prep_parts(g):
                n, h = g.n, g.h
                rows = listed[h]
                eng.wait_ge(act_look, 4 * (n + 1))
                eng.tensor_tensor(place[:, :, :], place_of[:, :].unsqueeze(2).broadcast_to([P, LISTS, GRAPHS]),
                                  rows[:, :, :, P + MORE], ALU.subtract).then_inc(dve_prep, 1)
                eng.wait_ge(dve_prep, at(PREP_DVE, n, "place"))
                eng.tensor_tensor(match[:, :, :], iota[:, 0:MORE].unsqueeze(1).broadcast_to([P, LISTS * GRAPHS, MORE]),
                                  place.rearrange("p l q -> p (l q)").unsqueeze(2)
                                  .broadcast_to([P, LISTS * GRAPHS, MORE]), ALU.is_equal).then_inc(dve_prep, 1)
                eng.wait_ge(dve_prep, at(PREP_DVE, n, "match"))
                eng.tensor_tensor(match[:, :, :], match[:, :, :],
                                  rows.rearrange("p l q r -> p (l q) r")[:, :, P:P + MORE], ALU.mult)\
                   .then_inc(dve_prep, 1)
                eng.wait_ge(dve_prep, at(PREP_DVE, n, "value"))
                for l in range(LISTS):
                    last = eng.reduce_sum(edge[h][:, :, l * (SLOTS - 1)], match[:, l * GRAPHS:(l + 1) * GRAPHS, :], AX.X)
                last.then_inc(dve_prep, 1)
                eng.wait_ge(dve_prep, at(PREP_DVE, n, "listed"))
                wait(eng, pe_turn, n - 1)
                parts_of(edge[h][:, :, :], parts[h], rest[:, :, :], dve_prep, PREP_DVE, n)
                eng.tensor_tensor(square[h][:, :, :], edge[h][:, :, :], edge[h][:, :, :], ALU.mult).then_inc(dve_prep, 1)

            def hots(g, q):
                u = GRAPHS * g.n + q
                if q == 0:
                    eng.wait_ge(dve_prep, at(PREP_DVE, g.n, "square"))
                wait(eng, pe_s[1], u - 1)
                for s in range(SLOTS):
                    row = A[g.h][:, q, :] if 0 < s < SLOTS - 1 else listed[g.h][:, s // DIRECT, q, 0:P]
                    last = eng.tensor_scalar(hot[q % 2][:, s, :], row, edge[g.h][:, q, s:s + 1],
                                             square[g.h][:, q, s:s + 1], ALU.is_equal, ALU.mult)
                last.then_inc(dve_hot, 1)

            def message(g, q, i):
                u = GRAPHS * g.n + q
                if q == 0 and i == 0:
                    eng.wait_ge(act_lrf, LISTS * (g.n + 1))
                eng.wait_ge(pe_w[i], u + 1)
                wait(eng, pe_s[i], u)
                eng.tensor_tensor(Z[i][:, :, :], (pW0, pW1)[i][:, 0:PAIRS * P].rearrange("p (a b) -> p a b", b=P),
                                  RF[g.h][:, q, i:i + PAIRS, :], ALU.mult).then_inc(dve_z[i], 1)

            def least_seen(g):
                eng.wait_ge(act_least, g.n + 1)
                eng.tensor_tensor(flags[:, 2, 0:1], flags[:, 2, 0:1], least[:, :], ALU.max).then_inc(dve_least, 1)

            def body(g, nxt, prev, later, ended):
                def tail(stage):
                    if prev:
                        tail_dve(eng, prev.n, stage)

                if not g:
                    tail_dve(eng, ended, "shift2")
                    for stage in ("degree", "soft", "sum1", "norm1", "sum2", "shift2"):
                        tail(stage)
                    return
                if nxt:
                    prep_left(nxt)
                message(g, 0, 0)
                if ended is not None:
                    tail_dve(eng, ended, "shift2")
                message(g, 0, 1)
                tail("degree")
                if nxt:
                    prep_more(nxt)
                hots(g, 1)

                message(g, 1, 0)
                tail("soft")
                if nxt:
                    prep_pick(nxt)
                message(g, 1, 1)
                hots(g, 2)
                tail("sum1")

                message(g, 2, 0)
                least_seen(g)
                tail("norm1")
                message(g, 2, 1)
                hots(g, 3)
                if nxt:
                    prep_parts(nxt)

                message(g, 3, 0)
                message(g, 3, 1)
                if nxt:
                    hots(nxt, 0)
                if later:
                    prep_top(later)
                tail("sum2")

            eng.memset(flags[:, :, :], 0.0).then_inc(s_bound, 1)
            for h in (0, 1):
                last = eng.memset(packed[h][:, :, :], 0.0)
            last.then_inc(s_bound, 1)
            eng.wait_ge(s_bound, 2)
            eng.wait_ge(s_const, 32)
            eng.tensor_scalar(B1L, B1, -LN2, None, ALU.add)
            eng.tensor_scalar(BD1N, BD1, -1.0, None, ALU.mult)
            eng.scalar_tensor_tensor(w1abs[:, :], W1, -1.0, W1, ALU.mult, ALU.max)
            eng.scalar_tensor_tensor(B1ABS, B1, -1.0, B1, ALU.mult, ALU.max).then_inc(s_bound, 1)
            first = Group(0, 0, 0)
            prep_top(first)
            prep_left(first)
            prep_more(first)
            eng.wait_ge(s_setup, 1)
            eng.tensor_copy(choose[:, :, :], chosen.rearrange("r q p a -> r (q p a)").unsqueeze(2)
                            .broadcast_to([P, GRAPHS * PAIRS * 2, NG])).then_inc(s_setup, 1)
            eng.wait_ge(s_count, 1)
            eng.tensor_tensor(BD2X[:, :], pM0[:, 0:P], BD2R, ALU.add).then_inc(s_bd2x, 1)
            prep_pick(first)
            prep_parts(first)
            eng.wait_ge(s_bound, 3)
            eng.reduce_sum(BOUND, w1abs[:, :], AX.X).then_inc(s_bound, 1)
            eng.wait_ge(s_bound, 4)
            eng.scalar_tensor_tensor(flags[:, 3, 0:1], BOUND, -SAFE, B1ABS, ALU.add, ALU.add)
            hots(first, 0)
            prep_top(Group(1, 0, 1))
            groups(eng, body)

            eng.wait_ge(dve_least, GROUPS)
            eng.reduce_max(worst[:, :], flags[:, :, :], AX.XY).then_inc(s_bound, 1)
            eng.wait_ge(s_bound, 5)
            eng.tensor_scalar(bad[:, :], worst[:, :], -1.0 if force_dense else 0.0, None, ALU.is_gt).then_inc(s_count, 1)
            eng.wait_ge(s_count, 3)
            eng.tensor_copy(verdict[:, :], pM1[0:1, 0:1]).then_inc(s_verdict, 1)
            eng.wait_ge(s_verdict, 1)
            flagged = eng.value_load(verdict[0:1, 0:1])
            with eng.If(flagged != 0):
                with eng.Fori(0, dense_groups) as n:
                    eng.wait_ge(dn_rfc, n + 1)
                    eng.memset(spare[:, :], 0.0)
                    with eng.Fori(0, GRAPHS) as q:
                        with eng.Fori(0, P // DENSE) as t:
                            k = (n * GRAPHS + q) * (P // DENSE) + t
                            some, width = slice(0, DENSE_PAIRS), DENSE_PAIRS * P
                            eng.wait_ge(d_block, 16 * (k + 1))
                            eng.tensor_tensor(square[0][:, 0, 0:DENSE], VB[:, :], VB[:, :], ALU.mult)
                            parts_of(VB[:, :], [x[:, 0, 0:DENSE] for x in parts[0]], VR[:, :], dn_dve, DENSE_DVE, k)
                            eng.wait_ge(dn_pe, at(DENSE_PE, k, "lin1"))
                            for i, pX in enumerate((pX0, pX1)):
                                last = eng.tensor_scalar(EX[i][:, some, :], pX[:, 0:width], B1, SAFE, ALU.add, ALU.min)
                            last.then_inc(dn_dve, 1)
                            eng.wait_ge(dn_act, at(DENSE_ACT, k, "log"))
                            for i, pX in enumerate((pX0, pX1)):
                                last = eng.scalar_tensor_tensor(H[i][:, some, :], pX[:, 0:width], B1L, EX[i][:, some, :],
                                                                ALU.add, ALU.max)
                            last.then_inc(dn_dve, 1)
                            eng.wait_ge(dn_pe, at(DENSE_PE, k, "lin2"))
                            for i, pW in enumerate((pW0, pW1)):
                                last = eng.tensor_tensor(Z[i][:, some, :],
                                                         pW[:, 0:width].rearrange("p (a b) -> p a b", b=P),
                                                         B2R.unsqueeze(1).broadcast_to([P, DENSE_PAIRS, P]), ALU.add)
                            last.then_inc(dn_dve, 1)
                            eng.wait_ge(dn_dve, at(DENSE_DVE, k, "shift"))
                            rf = RF[0].rearrange("p a b c -> p (a b c)")[:, bass.ds(q * 4 * P + P, P)]
                            for i in (0, 1):
                                last = eng.tensor_tensor(Z[i][:, some, :], Z[i][:, some, :],
                                                         rf.unsqueeze(1).broadcast_to([P, DENSE_PAIRS, P]), ALU.mult)
                            last.then_inc(dn_dve, 1)
                            eng.wait_ge(dn_pe, at(DENSE_PE, k, "y"))
                            eng.tensor_copy(YS.rearrange("p a b -> p (a b)")[:, bass.ds(q * P + t * DENSE, DENSE)],
                                            pY[:, 0:DENSE]).then_inc(dn_dve, 1)
                    eng.wait_ge(dn_dve, (n + 1) * (GRAPHS * P // DENSE) * len(DENSE_DVE))
                    eng.sem_inc(act_y, 1)
                    for stage in ("degree", "soft", "sum1", "norm1", "sum2", "shift2"):
                        tail_dve(eng, n + GROUPS, stage)

        @block.gpsimd
        def _(eng):
            def squares(g):
                eng.wait_ge(s_A[g.h], 16 * (g.half + 1))
                wait(eng, pe_share, GRAPHS * (g.n - 1))
                eng.tensor_tensor(A2[g.h][:, :, :], A[g.h][:, :, :], A[g.h][:, :, :], ALU.mult).then_inc(pool_sq, 1)

            def rfb(g):
                eng.wait_ge(act_rf, g.n + 1)
                wait(eng, pe_share, GRAPHS * g.n)
                eng.tensor_tensor(RFB[:, :, :], RF[g.h][:, :, 1, :], B2R.unsqueeze(1).broadcast_to([P, GRAPHS, P]),
                                  ALU.mult).then_inc(pool_rfb, 1)

            def adj_eye(g):
                wait(eng, pe_tail, at(TAIL_PE, g.n - 2, "spread"))
                eng.tensor_tensor(AI[g.h][:, :, :], A[g.h][:, :, :], ident[:, :].unsqueeze(1).broadcast_to([P, GRAPHS, P]),
                                  ALU.add).then_inc(pool_ai, 1)

            def body(g, nxt, prev, later, ended):
                def tail(stage):
                    if prev:
                        if stage == "base":
                            eng.wait_ge(s_XN, 16 * (prev.n + 1))
                        tail_pool(eng, prev.n, stage)

                if g:
                    rfb(g)
                tail("base")
                tail("dinv")
                if g:
                    adj_eye(g)
                if nxt:
                    squares(nxt)
                tail("rstd1")
                tail("scaled")
                tail("rstd2")

            eng.memset(ones[:, :], 1.0)
            eng.memset(halfc[:, :], 0.5)
            eng.memset(chosen[:, :, :, :], 0.0).then_inc(s_pool, 1)
            eng.memset(minus_half[:, :], -0.5)
            eng.memset(ident[:, :], 0.0).then_inc(s_pool, 1)
            eng.memset(before[:, :], 1.0).then_inc(s_pool, 1)
            eng.iota(iota[:, :], [[1, LISTS * P]], base=0, channel_multiplier=0, allow_small_or_imprecise_dtypes=True)
            eng.iota(place_of[:, :], [[P, LISTS]], base=0, channel_multiplier=1, allow_small_or_imprecise_dtypes=True)
            eng.wait_ge(s_pool, 3)
            eng.affine_select(out=ident[:, :], in_=ident[:, :], compare_op=ALU.not_equal, fill=1.0,
                              base=0, pattern=[[-1, P]], channel_multiplier=1).then_inc(s_pool, 1)
            eng.affine_select(out=before[:, :], in_=before[:, :], compare_op=ALU.is_gt, fill=0.0,
                              base=0, pattern=[[1, P]], channel_multiplier=-1)
            for i in range(3):
                eng.wait_ge(s_pool, 3 + i + (i > 0))
                eng.affine_select(out=chosen[:, :, :, :], in_=chosen[:, :, :, :], compare_op=ALU.not_equal, fill=1.0,
                                  base=-SLOTS * i, pattern=[[-BLOCK, GRAPHS], [-2, PAIRS], [-1, 2]],
                                  channel_multiplier=1).then_inc(s_pool, 1)
            eng.wait_ge(s_pool, 7)
            eng.tensor_copy(identb[:, :], ident[:, :]).then_inc(s_setup, 1)
            eng.wait_ge(s_const, 32)
            squares(Group(0, 0, 0))
            eng.wait_ge(s_bd2x, 1)
            groups(eng, body)

            eng.wait_ge(s_verdict, 1)
            flagged = eng.value_load(verdict[0:1, 0:1])
            with eng.If(flagged != 0):
                with eng.Fori(0, dense_groups) as n:
                    eng.wait_ge(d_in, 48 * (n + 1))
                    eng.tensor_tensor(AI[0][:, :, :], A[0][:, :, :], ident[:, :].unsqueeze(1).broadcast_to([P, GRAPHS, P]),
                                      ALU.add).then_inc(dn_ai, 1)
                    for stage in ("base", "dinv", "rstd1", "scaled", "rstd2"):
                        tail_pool(eng, n + GROUPS, stage)


def kernel(**inputs):
    import concourse.bacc as bacc
    from concourse.bass_utils import run_bass_kernel_spmd

    def by_node(a):
        return np.ascontiguousarray(a).reshape(P, B * P)

    i = {k: np.asarray(v) for k, v in inputs.items()}
    offsets = -np.linspace(0.0, CUTOFF, NG, dtype=np.float32)
    w1T = i["L0_gnn_W1"].T
    arrays = {
        "adjT": by_node(i["adj"].transpose(2, 0, 1)),
        "x_nodes": by_node(i["x"].transpose(1, 0, 2)),
        "x_features": by_node(i["x"].transpose(2, 0, 1)),
        "weights": np.ascontiguousarray(np.concatenate([
            np.concatenate([w1T, w1T]), i["L0_gnn_W2"].T, i["L0_gnn_Wa"].T, i["L0_gnn_Wd1"].T, i["L0_gnn_Wd2"].T,
            i["L1_gnn_weight"], i["L0_gnn_W1"], i["L0_gnn_b1"][:, None], i["L0_gnn_bd1"][:, None],
            np.concatenate([offsets, offsets])[:, None]], axis=1)),
        "biases": np.concatenate([i["L0_gnn_b2"], i["L0_gnn_bd2"], i["L1_gnn_bias"]]).reshape(1, 3 * P),
    }
    nc = bacc.Bacc("TRN2", target_bir_lowering=False, num_devices=1)
    args = [nc.dram_tensor(n, a.shape, mybir.dt.from_np(a.dtype), kind="ExternalInput").ap() for n, a in arrays.items()]
    out = nc.dram_tensor("out_nodes", (P, B * P), mybir.dt.float32, kind="ExternalOutput").ap()
    gnn_kernel(nc, *args, out)
    r = run_bass_kernel_spmd(nc, [arrays], core_ids=[0])
    return np.ascontiguousarray(r.results[0]["out_nodes"].reshape(P, B, P).transpose(1, 0, 2))
```

```python
import math
from collections import namedtuple
from contextlib import ExitStack

import numpy as np

import concourse.bass as bass
from concourse import mybir

B, P, NG = 64, 128, 64
CUTOFF = 5.0
LN2 = math.log(2.0)
EPS = 1e-5
GRAPHS = 4
GROUPS = B // GRAPHS
DIRECT = 4
LISTS = 2
SLOTS = LISTS + DIRECT
PAIRS = SLOTS // 2
TOP = 8
MORE = 2 * TOP
W = GRAPHS * P
BLOCK = P // GRAPHS
ROW = P + MORE + 1
PART = 2
LOOKS = LISTS * GRAPHS // PART
SAFE = 30.0

PREP_DVE = ["top", "differ", "edge", "left1", "more1", "left2", "more2", "differ2", "found", "lane",
            "count", "base", "end", "from", "pick", "place", "match", "value", "listed",
            "hi", "rest", "mid", "lo", "square"]
TAIL_PE = ["lin1", "lin2", "spread", "out"]
TAIL_DVE = ["soft", "sum1", "stats1", "moments1", "shift1",
            "sum2", "stats2", "moments2", "shift2"]
TAIL_ACT = ["abs", "exp", "log", "spread"]
DEGREE_POOL = ["root", "power", "dinv"]
TAIL_POOL = ["base", "var1", "rstd1", "scaled", "biased", "var2", "rstd2"]
DENSE = 4
DENSE_PAIRS = DENSE // 2
DENSE_PE = ["turn", "edge", "lin1", "lin2", "y"]
DENSE_DVE = ["hi", "rest", "mid", "lo", "clamp", "soft", "shift", "msg", "y"]
DENSE_ACT = ["turn", "square", "gauss", "exp", "log"]

WEIGHTS = 6 * P + NG + 3

Group = namedtuple("Group", "n half h")


def at(names, n, name):
    return n * len(names) + names.index(name) + 1


def wait(eng, sem, value):
    if not isinstance(value, int) or value > 0:
        eng.wait_ge(sem, value)


def gnn_kernel(nc, adjT, adj, x, xT, weights, biases, out,
               force_dense=False, dense_groups=GROUPS):
    f32, bf16, i32 = mybir.dt.float32, mybir.dt.bfloat16, mybir.dt.int32
    ALU, ACT, AX = mybir.AluOpType, mybir.ActivationFunctionType, mybir.AxisListType
    width = np.linspace(0.0, CUTOFF, NG, dtype=np.float32)
    width = np.float32(width[1] - width[0])
    COEFF = float(np.float32(-0.5) / (width * width))

    with ExitStack() as ctx:
        def sb(name, shape, dt=f32):
            return ctx.enter_context(nc.sbuf_tensor(name, shape, dt))

        def pb(name):
            return ctx.enter_context(nc.psum_tensor(name, [P, W], f32))

        def sem(name):
            return ctx.enter_context(nc.semaphore(name))

        CW = sb("all_weights", [P, WEIGHTS])
        W1T, W2T, WAT, WD1T, WD2T, WG = (CW[:, bass.ts(i, P)] for i in range(6))
        W1 = CW[:, 6 * P:6 * P + NG]
        B1, BD1, NOFF = (CW[:, 6 * P + NG + i:6 * P + NG + i + 1] for i in range(3))
        CB = sb("all_biases", [P, 3 * P])
        B2R, BD2R, BGR = (CB[:, bass.ts(i, P)] for i in range(3))
        cols = sb("cols", [P, 4])
        B1L, BD1N, BOUND, B1ABS = (cols[:, i:i + 1] for i in range(4))
        BD2X = sb("BD2X", [P, P])
        ident, identb = sb("ident", [P, P]), sb("identb", [P, P], bf16)
        before, iota, place_of = sb("before", [P, P]), sb("iota", [P, LISTS * P]), sb("place_of", [P, LISTS])
        ones, minus_half = sb("ones", [P, 1]), sb("minus_half", [P, GRAPHS])
        epsilon = sb("epsilon", [P, GRAPHS])
        w1abs = sb("w1abs", [P, NG])
        halfc = sb("halfc", [P, 1])

        rows = [sb(f"rows{h}", [P, GRAPHS, ROW]) for h in (0, 1)]
        A = [rows[h][:, :, 0:P] for h in (0, 1)]
        XT = [sb(f"XT{h}", [P, GRAPHS, P]) for h in (0, 1)]
        XN = sb("XN", [P, GRAPHS, P])
        top = sb("top", [P, GRAPHS, TOP])
        differ = sb("differ", [P, GRAPHS, DIRECT])
        edge = [sb(f"edge{h}", [P, GRAPHS, SLOTS]) for h in (0, 1)]
        square = [sb(f"square{h}", [P, GRAPHS, SLOTS]) for h in (0, 1)]
        rest = sb("rest", [P, GRAPHS, SLOTS])
        packed = [sb(f"packed{h}", [P, GRAPHS, BLOCK], bf16) for h in (0, 1)]
        parts = [[packed[h][:, :, i * SLOTS:(i + 1) * SLOTS] for i in range(3)] for h in (0, 1)]
        turned = sb("turned", [P, P], bf16)
        chosen = sb("chosen", [P, GRAPHS, PAIRS, 2], bf16)
        choose = sb("choose", [P, GRAPHS * PAIRS * 2, NG], bf16)
        more, left = sb("more", [P, GRAPHS, MORE]), sb("left", [P, GRAPHS, P])
        differ2, found = sb("differ2", [P, GRAPHS, MORE]), sb("found", [P, GRAPHS, MORE])
        count, span_end = sb("count", [P, GRAPHS]), sb("span_end", [P, GRAPHS])
        started, pick = sb("started", [P, GRAPHS, LISTS * P]), sb("pick", [P, GRAPHS, LISTS * P])
        listed = [sb(f"listed{h}", [P, LISTS, GRAPHS, ROW]) for h in (0, 1)]
        place = sb("place", [P, LISTS, GRAPHS])
        match = sb("match", [P, LISTS * GRAPHS, MORE])
        flags = sb("flags", [P, 4, GRAPHS])
        least, unused = sb("least", [P, 1]), sb("unused", [P, GRAPHS, P])
        RF = [sb(f"RF{h}", [P, GRAPHS, LISTS + 1, P]) for h in (0, 1)]
        RFB = sb("RFB", [P, GRAPHS, P])
        A2 = [sb(f"A2{h}", [P, GRAPHS, P]) for h in (0, 1)]
        AI = [sb(f"AI{h}", [P, GRAPHS, P]) for h in (0, 1)]
        hot = [sb(f"hot{h}", [P, SLOTS, P]) for h in (0, 1)]
        DIFF2, G = sb("DIFF2", [P, PAIRS, P]), sb("G", [P, PAIRS, P])
        EX = [sb(f"EX{i}", [P, PAIRS, P]) for i in (0, 1)]
        H = [sb(f"H{i}", [P, PAIRS, P]) for i in (0, 1)]
        Z = [sb(f"Z{i}", [P, PAIRS, P]) for i in (0, 1)]
        YS, UC, S1 = (sb(n, [P, GRAPHS, P]) for n in ("YS", "UC", "S1"))
        UE, UL, XB, R1, X1 = (sb(n, [P, GRAPHS, P]) for n in ("UE", "UL", "XB", "R1", "X1"))
        XS, X1B, SP, R2 = (sb(n, [P, GRAPHS, P]) for n in ("XS", "X1B", "SP", "R2"))
        OUT = sb("OUT", [P, GRAPHS, P])
        AR, deg = sb("AR", [P, GRAPHS, P]), sb("deg", [P, 2, 6, GRAPHS])
        SUMS, DEG0, DEG1, DEGN, ROOT, DINV = ([deg[:, h, i, :] for h in (0, 1)] for i in range(6))
        stats = sb("stats", [P, GRAPHS, 6])
        mv = [sb(f"mv{i}", [P, GRAPHS, 2]) for i in (0, 1)]
        var = [sb(f"var{i}", [P, GRAPHS]) for i in (0, 1)]
        rstd = [sb(f"rstd{i}", [P, GRAPHS]) for i in (0, 1)]
        shift = [sb(f"shift{i}", [P, GRAPHS]) for i in (0, 1)]
        spare = sb("spare", [P, 5])
        worst, bad, verdict = sb("worst", [P, 1]), sb("bad", [P, 1]), sb("verdict", [1, 1], i32)
        VB, VR = sb("VB", [P, DENSE]), sb("VR", [P, DENSE])

        pE, pX0, pX1, pW0, pW1, pY, pM0, pM1 = (pb(n) for n in ("pE", "pX0", "pX1", "pW0", "pW1", "pY", "pM0", "pM1"))

        s_const, s_setup = sem("consts_loaded"), sem("consts_made")
        s_A = [sem(f"adj_loaded{h}") for h in (0, 1)]
        s_XT = [sem(f"xT_loaded{h}") for h in (0, 1)]
        s_XN, s_AR, s_out = sem("x_loaded"), sem("adj_rows_loaded"), sem("out_stored")
        pe_e, pe_x = sem("edges_spread"), [sem(f"lin1_done{i}") for i in (0, 1)]
        pe_share, s_bd2x = sem("b2_share_done"), sem("second_bias_done")
        pe_w, pe_s = [sem(f"filter_done{i}") for i in (0, 1)], [sem(f"summed{i}") for i in (0, 1)]
        act_e, act_g = sem("diff_squared"), sem("gauss_done")
        act_x, act_h = [sem(f"exp_done{i}") for i in (0, 1)], [sem(f"soft_done{i}") for i in (0, 1)]
        dve_hot, dve_z = sem("hot_done"), [sem(f"message_done{i}") for i in (0, 1)]
        dve_prep = sem("prep_dve")
        pe_rf, act_rf, pe_base = sem("rf_done"), sem("rf_copied"), sem("starts_done")
        pe_look, act_look = sem("looked_up"), sem("listed_copied")
        pe_turn, act_turned = sem("parts_turned"), sem("turned_copied")
        pe_lrf, act_lrf = sem("list_rf_done"), sem("list_rf_copied")
        pool_sq, pool_rfb, pool_ai = sem("squares_done"), sem("rfb_done"), sem("adj_eye_done")
        act_least, dve_least = sem("negatives_summed"), sem("negatives_noted")
        act_degree, dve_degree, pool_degree = sem("degree_act"), sem("degree_dve"), sem("degree_pool")
        act_y, act_norm, act_out = sem("y_copied"), sem("norm1_done"), sem("out_done")
        pe_tail, dve_tail, act_tail, pool_tail = sem("tail_pe"), sem("tail_dve"), sem("tail_act"), sem("tail_pool")
        s_verdict, s_count, s_bound, s_pool = sem("verdict"), sem("bad_counted"), sem("bound_done"), sem("pool_consts")
        d_in, d_block, d_store = sem("dense_in"), sem("dense_block"), sem("dense_stored")
        dn_pe, dn_dve, dn_act = sem("dense_pe"), sem("dense_dve"), sem("dense_act")
        dn_rf, dn_rfc, dn_ai, dn_free = sem("dense_rf"), sem("dense_rf_copied"), sem("dense_adj_eye"), sem("dense_block_free")

        block = ctx.enter_context(nc.Block())

        def groups(eng, body):
            def step(n, half, h):
                first, left = isinstance(n, int) and n == 0, GROUPS - 1 - n if isinstance(n, int) else GROUPS
                body(Group(n, half, h), Group(n + 1, half + h, 1 - h) if left > 0 else None,
                     None if first else Group(n - 1, half - 1 + h, 1 - h),
                     Group(n + 2, half + 1, h) if left > 1 else None,
                     n - 2 if not isinstance(n, int) or n > 1 else None)

            step(0, 0, 0)
            step(1, 0, 1)
            with eng.Fori(0, GROUPS // 2 - 2) as t:
                step(2 * t + 2, t + 1, 0)
                step(2 * t + 3, t + 1, 1)
            step(GROUPS - 2, GROUPS // 2 - 1, 0)
            step(GROUPS - 1, GROUPS // 2 - 1, 1)
            body(None, None, Group(GROUPS - 1, GROUPS // 2 - 1, 1), None, GROUPS - 2)

        @block.sync
        def _(eng):
            def store(c):
                eng.wait_ge(act_out, c + 1)
                eng.dma_start(out[:, bass.ds(c * W, W)], OUT[:, :, :]).then_inc(s_out, 16)

            def load_adj(g, n):
                eng.dma_start(A[g.h], adjT[:, bass.ds(n * W, W)]).then_inc(s_A[g.h], 16)

            def load_xT(g, n):
                eng.dma_start(XT[g.h][:, :, :], xT[:, bass.ds(n * W, W)]).then_inc(s_XT[g.h], 16)

            def body(g, nxt, prev, later, ended):
                if g:
                    n = g.n
                    if later:
                        wait(eng, pe_rf, n + 1)
                        load_xT(g, n + 2)
                    if prev:
                        wait(eng, pool_tail, at(TAIL_POOL, n - 1, "base"))
                    eng.dma_start(XN[:, :, :], x[:, bass.ds(n * W, W)]).then_inc(s_XN, 16)
                    wait(eng, act_degree, n)
                    eng.dma_start(AR[:, :, :], adj[:, bass.ds(n * W, W)]).then_inc(s_AR, 16)
                if later:
                    eng.wait_ge(dve_hot, GRAPHS * (n + 1))
                    eng.wait_ge(pool_ai, n + 1)
                    eng.wait_ge(act_least, n + 1)
                    load_adj(g, n + 2)
                if ended is not None:
                    store(ended)
                if not g:
                    store(prev.n)

            eng.sem_inc(s_out, 16)
            load_adj(Group(0, 0, 0), 0)
            load_xT(Group(0, 0, 0), 0)
            eng.dma_start(CW[:, :], weights).then_inc(s_const, 16)
            eng.dma_start(CB[:, :], biases.broadcast_to([P, 3 * P])).then_inc(s_const, 16)
            load_adj(Group(1, 0, 1), 1)
            load_xT(Group(1, 0, 1), 1)
            groups(eng, body)
            eng.wait_ge(s_out, 16 * (GROUPS + 1))

            eng.wait_ge(s_verdict, 1)
            flagged = eng.value_load(verdict[0:1, 0:1])
            with eng.If(flagged != 0):
                with eng.Fori(0, dense_groups) as n:
                    eng.dma_start(A[0], adjT[:, bass.ds(n * W, W)]).then_inc(d_in, 16)
                    eng.dma_start(AR[:, :, :], adj[:, bass.ds(n * W, W)]).then_inc(d_in, 16)
                    eng.dma_start(XT[0][:, :, :], xT[:, bass.ds(n * W, W)]).then_inc(d_in, 16)
                    eng.dma_start(XN[:, :, :], x[:, bass.ds(n * W, W)]).then_inc(d_in, 16)
                    with eng.Fori(0, GRAPHS) as q:
                        with eng.Fori(0, P // DENSE) as t:
                            k = (n * GRAPHS + q) * (P // DENSE) + t
                            eng.dma_start(VB[:, :], adjT[:, bass.ds(n * W + q * P + t * DENSE, DENSE)]).then_inc(d_block, 16)
                            eng.wait_ge(dn_dve, (k + 1) * len(DENSE_DVE))
                            eng.sem_inc(dn_free, 1)
                    eng.wait_ge(act_out, n + GROUPS + 1)
                    eng.dma_start(out[:, bass.ds(n * W, W)], OUT[:, :, :]).then_inc(d_store, 16)
                    eng.wait_ge(d_store, 16 * (n + 1))
                    eng.sem_inc(dn_free, 1)

        def degree_act(eng, n, h, q):
            done = eng.activation(unused[:, q, :], AR[:, q, :], ACT.Copy, accum_out=SUMS[h][:, q:q + 1])
            if q == GRAPHS - 1:
                done.then_inc(act_degree, 1)

        def degree_dve(eng, n, h):
            eng.wait_ge(act_degree, n + 1)
            eng.tensor_scalar(DEG0[h], SUMS[h], 1.0, 0.0, ALU.add, ALU.is_equal)
            eng.tensor_scalar(DEGN[h], SUMS[h], 1.0, 0.0, ALU.add, ALU.not_equal)
            eng.tensor_scalar(DEG1[h], SUMS[h], 1.0, None, ALU.add).then_inc(dve_degree, 1)

        def degree_pool(eng, n, h):
            eng.wait_ge(dve_degree, n + 1)
            eng.tensor_tensor(ROOT[h], DEG1[h], DEG0[h], ALU.add).then_inc(pool_degree, 1)
            eng.wait_ge(pool_degree, at(DEGREE_POOL, n, "root"))
            eng.tensor_tensor(ROOT[h], ROOT[h], minus_half[:, :], ALU.pow).then_inc(pool_degree, 1)
            eng.wait_ge(pool_degree, at(DEGREE_POOL, n, "power"))
            eng.tensor_tensor(DINV[h], ROOT[h], DEGN[h], ALU.mult).then_inc(pool_degree, 1)

        def tail_pe(eng, c, h, stage):
            if stage == "lin1":
                eng.wait_ge(act_y, c + 1)
                wait(eng, dve_tail, at(TAIL_DVE, c - 1, "sum2"))
                eng.matmul(pM0[:, :], WD1T, YS[:, :, :], start=True, stop=True).then_inc(pe_tail, 1)
            if stage == "lin2":
                eng.wait_ge(dve_tail, at(TAIL_DVE, c, "soft"))
                for q in range(GRAPHS):
                    last = eng.matmul(pM0[:, bass.ts(q, P)], S1[:, q, :], WD2T, start=True, stop=True)
                last.then_inc(pe_tail, 1)
            if stage == "spread":
                eng.wait_ge(pool_tail, at(TAIL_POOL, c, "scaled"))
                for q in range(GRAPHS):
                    last = eng.matmul(pM0[:, bass.ts(q, P)], XS[:, q, :], AI[h][:, q, :], start=True, stop=True)
                last.then_inc(pe_tail, 1)
            if stage == "out":
                eng.wait_ge(act_tail, at(TAIL_ACT, c, "spread"))
                for q in range(GRAPHS):
                    last = eng.matmul(pM0[:, bass.ts(q, P)], SP[:, q, :], WG, start=True, stop=True)
                last.then_inc(pe_tail, 1)

        def tail_act(eng, c, stage):
            if stage == "soft":
                eng.wait_ge(pe_tail, at(TAIL_PE, c, "lin1"))
                eng.activation(UC[:, :, :], pM0[:, :], ACT.Abs, bias=BD1).then_inc(act_tail, 1)
                eng.wait_ge(act_tail, at(TAIL_ACT, c, "abs"))
                eng.activation(UE[:, :, :], UC[:, :, :], ACT.Exp, scale=-1.0).then_inc(act_tail, 1)
                eng.wait_ge(act_tail, at(TAIL_ACT, c, "exp"))
                wait(eng, dve_tail, at(TAIL_DVE, c - 1, "soft"))
                eng.activation(UL[:, :, :], UE[:, :, :], ACT.Ln, bias=halfc[:, :], scale=0.5).then_inc(act_tail, 1)
            if stage == "spread":
                eng.wait_ge(pe_tail, at(TAIL_PE, c, "spread"))
                eng.activation(SP[:, :, :], pM0[:, :], ACT.Copy).then_inc(act_tail, 1)
            if stage in ("norm1", "norm2"):
                i = int(stage[-1]) - 1
                eng.wait_ge(dve_tail, at(TAIL_DVE, c, f"shift{i + 1}"))
                if i == 0:
                    wait(eng, pool_tail, at(TAIL_POOL, c - 1, "biased"))
                for q in range(GRAPHS):
                    last = eng.activation((X1, OUT)[i][:, q, :], (R1, R2)[i][:, q, :], ACT.Identity,
                                          bias=shift[i][:, q:q + 1], scale=rstd[i][:, q:q + 1])
                last.then_inc((act_norm, act_out)[i], 1)

        def tail_dve(eng, c, h, stage):
            if stage == "soft":
                eng.wait_ge(act_tail, at(TAIL_ACT, c, "log"))
                eng.scalar_tensor_tensor(S1[:, :, :], pM0[:, :], BD1N, UL[:, :, :], ALU.max, ALU.add).then_inc(dve_tail, 1)
            if stage == "sum1":
                eng.wait_ge(pe_tail, at(TAIL_PE, c, "lin2"))
                eng.wait_ge(pool_tail, at(TAIL_POOL, c, "base"))
                wait(eng, act_norm, c)
                eng.tensor_tensor(R1[:, :, :], pM0[:, :], XB[:, :, :], ALU.add).then_inc(dve_tail, 1)
            if stage == "sum2":
                eng.wait_ge(pe_tail, at(TAIL_PE, c, "out"))
                wait(eng, act_out, c)
                eng.wait_ge(pool_tail, at(TAIL_POOL, c, "biased"))
                for q in range(GRAPHS):
                    last = eng.scalar_tensor_tensor(R2[:, q, :], pM0[:, bass.ts(q, P)], DINV[h][:, q:q + 1],
                                                    X1B[:, q, :], ALU.mult, ALU.add)
                last.then_inc(dve_tail, 1)
            if stage in ("stats1", "stats2"):
                eng.wait_ge(dve_tail, at(TAIL_DVE, c, stage) - 1)
                for q in range(GRAPHS):
                    last = eng.bn_stats(stats[:, q, :], (R1, R2)[stage == "stats2"][:, q, :])
                last.then_inc(dve_tail, 1)
            if stage in ("moments1", "moments2"):
                eng.wait_ge(dve_tail, at(TAIL_DVE, c, stage) - 1)
                eng.memset(spare[:, 3:4], 0.0)
                for q in range(GRAPHS):
                    last = eng.bn_aggr(mv[stage == "moments2"][:, q, :], stats[:, q, :])
                last.then_inc(dve_tail, 1)
            if stage in ("shift1", "shift2"):
                i = int(stage[-1]) - 1
                eng.wait_ge(pool_tail, at(TAIL_POOL, c, f"rstd{i + 1}"))
                eng.scalar_tensor_tensor(shift[i][:, :], mv[i][:, :, 0], -1.0, rstd[i][:, :], ALU.mult, ALU.mult)\
                   .then_inc(dve_tail, 1)

        def tail_pool(eng, c, h, stage):
            if stage == "base":
                wait(eng, dve_tail, at(TAIL_DVE, c - 1, "sum1"))
                eng.tensor_tensor(XB[:, :, :], XN[:, :, :], BD2X[:, :].unsqueeze(1).broadcast_to([P, GRAPHS, P]),
                                  ALU.add).then_inc(pool_tail, 1)
            if stage in ("rstd1", "rstd2"):
                i = int(stage[-1]) - 1
                eng.wait_ge(dve_tail, at(TAIL_DVE, c, f"moments{i + 1}"))
                eng.tensor_tensor(var[i][:, :], mv[i][:, :, 1], epsilon[:, :], ALU.add).then_inc(pool_tail, 1)
                eng.wait_ge(pool_tail, at(TAIL_POOL, c, f"var{i + 1}"))
                eng.tensor_tensor(rstd[i][:, :], var[i][:, :], minus_half[:, :], ALU.pow).then_inc(pool_tail, 1)
            if stage == "scaled":
                eng.wait_ge(act_norm, c + 1)
                eng.wait_ge(pool_degree, at(DEGREE_POOL, c, "dinv"))
                eng.tensor_tensor(XS[:, :, :], X1[:, :, :], DINV[h].unsqueeze(2).broadcast_to([P, GRAPHS, P]),
                                  ALU.mult).then_inc(pool_tail, 1)
                eng.tensor_tensor(X1B[:, :, :], X1[:, :, :], BGR.unsqueeze(1).broadcast_to([P, GRAPHS, P]),
                                  ALU.add).then_inc(pool_tail, 1)

        def spread_edges(eng, q, pairs=PAIRS):
            for p in range(pairs):
                k = (q * PAIRS + p) * 2
                last = eng.matmul(pE[:, bass.ts(p, P)], choose[:, k:k + 2, :], turned[:, :], start=True, stop=True)
            return last

        @block.tensor
        def _(eng):
            def project(g):
                eng.wait_ge(s_XT[g.h], 16 * (g.half + 1))
                wait(eng, act_lrf, LISTS * g.n)
                for q in range(GRAPHS):
                    last = eng.matmul(pM1[:, bass.ts(q, P)], XT[g.h][:, q, :], WAT, start=True, stop=True)
                last.then_inc(pe_rf, 1)

            def starts(g):
                eng.wait_ge(dve_prep, at(PREP_DVE, g.n, "count"))
                eng.wait_ge(act_rf, g.n + 1)
                eng.matmul(pM1[:, 0:GRAPHS], before[:, :], count[:, :], start=True, stop=True).then_inc(pe_base, 1)

            def look_up(g, k, bank=None):
                if k == 0:
                    eng.wait_ge(dve_prep, at(PREP_DVE, g.n, "pick"))
                wait(eng, act_look, LOOKS * g.n + k - (bank is not None))
                for j in range(PART):
                    q = PART * (k % 2) + j
                    last = eng.matmul((bank or pM1)[:, bass.ts(j, ROW)], pick[:, q, bass.ts(k // 2, P)], rows[g.h][:, q, :],
                                      start=True, stop=True)
                last.then_inc(pe_look, 1)

            def turn(g):
                eng.wait_ge(dve_prep, at(PREP_DVE, g.n, "lo"))
                eng.matmul(pM1[:, 0:P], packed[g.h][:, :, :], identb[:, :], start=True, stop=True).then_inc(pe_turn, 1)

            def list_rf(g, l, bank=None):
                if not bank:
                    eng.wait_ge(act_turned, g.n + 1)
                    wait(eng, act_lrf, LISTS * g.n + l)
                for q in range(GRAPHS):
                    last = eng.matmul((bank or pM1)[:, bass.ts(q, P)], pick[:, q, bass.ts(l, P)], RF[g.h][:, q, LISTS, :],
                                      start=True, stop=True)
                last.then_inc(pe_lrf, 1)

            def spread(g, q):
                u = GRAPHS * g.n + q
                if q == 0:
                    eng.wait_ge(act_turned, g.n + 1)
                wait(eng, act_e, u)
                spread_edges(eng, q).then_inc(pe_e, 1)

            def lin1(g, q):
                u = GRAPHS * g.n + q
                eng.wait_ge(act_g, u + 1)
                wait(eng, act_x[0], u)
                wait(eng, act_x[1], u)
                eng.matmul(pX0[:, 0:PAIRS * P], W1T[0:NG, :], G[0:NG, :, :], start=True, stop=True).then_inc(pe_x[0], 1)
                eng.matmul(pX1[:, 0:PAIRS * P], W1T[NG:P, :], G[NG:P, :, :], start=True, stop=True).then_inc(pe_x[1], 1)

            def lin2(g, q, i):
                u = GRAPHS * g.n + q
                eng.wait_ge(act_h[i], u + 1)
                wait(eng, dve_z[i], u)
                for p in range(PAIRS):
                    last = eng.matmul((pW0, pW1)[i][:, bass.ts(p, P)], H[i][:, p, :], W2T, start=True, stop=True)
                last.then_inc(pe_w[i], 1)

            def shared(g, q):
                if q == 0:
                    eng.wait_ge(pool_rfb, g.n + 1)
                    eng.wait_ge(pool_sq, g.n + 1)
                    wait(eng, act_y, g.n)
                eng.matmul(pY[:, bass.ts(q, P)], RFB[:, q, :], A2[g.h][:, q, :], start=q == 0, stop=False,
                           skip_group_check=True).then_inc(pe_share, 1)

            def messages(g, q, i):
                u = GRAPHS * g.n + q
                if i == 0:
                    eng.wait_ge(dve_hot, u + 1)
                eng.wait_ge(dve_z[i], u + 1)
                for p in range(PAIRS):
                    last = eng.matmul(pY[:, bass.ts(q, P)], Z[i][:, p, :], hot[q % 2][:, PAIRS * i + p, :],
                                      start=False, stop=False, skip_group_check=True)
                last.then_inc(pe_s[i], 1)

            def body(g, nxt, prev, later, ended):
                def tail(stage):
                    if prev:
                        tail_pe(eng, prev.n, prev.h, stage)

                if not g:
                    for stage in TAIL_PE:
                        tail(stage)
                    return
                lin2(g, 0, 0)
                lin2(g, 0, 1)
                if nxt:
                    project(nxt)
                lin1(g, 1)
                spread(g, 2)
                tail("lin1")
                shared(g, 0)
                if nxt:
                    starts(nxt)
                messages(g, 0, 0)
                messages(g, 0, 1)

                lin2(g, 1, 0)
                lin1(g, 2)
                spread(g, 3)
                lin2(g, 1, 1)
                if nxt:
                    look_up(nxt, 0)
                shared(g, 1)
                messages(g, 1, 0)
                messages(g, 1, 1)
                if nxt:
                    look_up(nxt, 1)
                tail("lin2")

                lin2(g, 2, 0)
                lin1(g, 3)
                if nxt:
                    look_up(nxt, 2)
                lin2(g, 2, 1)
                shared(g, 2)
                if nxt:
                    look_up(nxt, 3)
                messages(g, 2, 0)
                messages(g, 2, 1)

                lin2(g, 3, 0)
                lin2(g, 3, 1)
                shared(g, 3)
                if nxt:
                    turn(nxt)
                tail("spread")
                messages(g, 3, 0)
                if nxt:
                    spread(nxt, 0)
                if nxt:
                    list_rf(nxt, 0)
                messages(g, 3, 1)
                if nxt:
                    lin1(nxt, 0)
                tail("out")
                if nxt:
                    list_rf(nxt, 1)
                    spread(nxt, 1)

            eng.wait_ge(s_const, 32)
            first = Group(0, 0, 0)
            project(first)
            eng.matmul(pM0[:, 0:P], BD1.broadcast_to([P, P]), WD2T, start=True, stop=True).then_inc(s_count, 1)
            eng.wait_ge(s_setup, 1)
            starts(first)
            for k in range(LOOKS):
                look_up(first, k, (pW0, pW1)[k % 2])
            for l in range(LISTS):
                list_rf(first, l, (pX0, pX1)[l])
            eng.wait_ge(s_setup, 2)
            turn(first)
            spread(first, 0)
            lin1(first, 0)
            spread(first, 1)
            groups(eng, body)

            eng.wait_ge(s_count, 2)
            eng.matmul(pM1[0:1, 0:1], bad[:, :], ones[:, :], start=True, stop=True).then_inc(s_count, 1)
            eng.wait_ge(s_verdict, 1)
            flagged = eng.value_load(verdict[0:1, 0:1])
            with eng.If(flagged != 0):
                with eng.Fori(0, dense_groups) as n:
                    eng.wait_ge(d_in, 64 * (n + 1))
                    for q in range(GRAPHS):
                        last = eng.matmul(pM1[:, bass.ts(q, P)], XT[0][:, q, :], WAT, start=True, stop=True)
                    last.then_inc(dn_rf, 1)
                    with eng.Fori(0, GRAPHS * P // DENSE) as m:
                        k = n * (GRAPHS * P // DENSE) + m
                        eng.wait_ge(dn_dve, at(DENSE_DVE, k, "lo"))
                        eng.matmul(pW0[:, 0:P], packed[0][:, :, :], identb[:, :], start=True, stop=True).then_inc(dn_pe, 1)
                        eng.wait_ge(dn_act, at(DENSE_ACT, k, "turn"))
                        spread_edges(eng, 0, DENSE_PAIRS).then_inc(dn_pe, 1)
                        eng.wait_ge(dn_act, at(DENSE_ACT, k, "gauss"))
                        width = DENSE_PAIRS * P
                        eng.matmul(pX0[:, 0:width], W1T[0:NG, :], G[0:NG, 0:DENSE_PAIRS, :], start=True, stop=True)
                        eng.matmul(pX1[:, 0:width], W1T[NG:P, :], G[NG:P, 0:DENSE_PAIRS, :], start=True, stop=True)\
                           .then_inc(dn_pe, 1)
                        eng.wait_ge(dn_dve, at(DENSE_DVE, k, "soft"))
                        for i in (0, 1):
                            for p in range(DENSE_PAIRS):
                                last = eng.matmul((pW0, pW1)[i][:, bass.ts(p, P)], H[i][:, p, :], W2T,
                                                  start=True, stop=True)
                        last.then_inc(dn_pe, 1)
                        eng.wait_ge(dn_dve, at(DENSE_DVE, k, "msg"))
                        for s in range(DENSE):
                            last = eng.matmul(pY[:, s:s + 1], Z[s // DENSE_PAIRS][:, s % DENSE_PAIRS, :], square[0][:, 0, s:s + 1],
                                              start=True, stop=True)
                        last.then_inc(dn_pe, 1)
                    eng.wait_ge(dn_ai, n + 1)
                    for stage in TAIL_PE:
                        tail_pe(eng, n + GROUPS, 0, stage)

        @block.scalar
        def _(eng):
            def squares(g, q):
                u = GRAPHS * g.n + q
                eng.wait_ge(pe_e, u + 1)
                eng.activation(DIFF2[:, :, :], pE[:, 0:PAIRS * P], ACT.Square, bias=NOFF).then_inc(act_e, 1)
                eng.wait_ge(act_e, u + 1)
                wait(eng, pe_x[1], u)
                eng.activation(G[:, :, :], DIFF2[:, :, :], ACT.Exp, scale=COEFF).then_inc(act_g, 1)

            def soft(g, q, i):
                u = GRAPHS * g.n + q
                eng.wait_ge(pe_x[i], u + 1)
                eng.activation(EX[i][:, :, :], (pX0, pX1)[i][:, 0:PAIRS * P], ACT.Exp, bias=B1).then_inc(act_x[i], 1)
                eng.wait_ge(act_x[i], u + 1)
                wait(eng, pe_w[i], u)
                eng.activation(H[i][:, :, :], EX[i][:, :, :], ACT.Ln, bias=halfc[:, :], scale=0.5).then_inc(act_h[i], 1)

            def copy_rf(g):
                eng.wait_ge(pe_rf, g.n + 1)
                wait(eng, dve_z[1], GRAPHS * (g.n - 1))
                wait(eng, pool_rfb, g.n - 1)
                eng.activation(RF[g.h][:, :, LISTS, :], pM1[:, :].rearrange("p (a b) -> p a b", b=P), ACT.Copy)\
                   .then_inc(act_rf, 1)

            def copy_list_rf(g, l, bank=pM1):
                eng.wait_ge(pe_lrf, LISTS * g.n + l + 1)
                eng.activation(RF[g.h][:, :, l, :], bank[:, :].rearrange("p (a b) -> p a b", b=P), ACT.Copy)\
                   .then_inc(act_lrf, 1)

            def copy_listed(g, k, bank=pM1):
                eng.wait_ge(pe_look, LOOKS * g.n + k + 1)
                wait(eng, dve_hot, GRAPHS * (g.n - 1))
                q = PART * (k % 2)
                eng.activation(listed[g.h][:, k // 2, q:q + PART, :],
                               bank[:, 0:PART * ROW].rearrange("p (a b) -> p a b", b=ROW), ACT.Copy).then_inc(act_look, 1)

            def copy_turned(g):
                eng.wait_ge(pe_turn, g.n + 1)
                eng.activation(turned[:, :], pM1[:, 0:P], ACT.Copy).then_inc(act_turned, 1)

            def copy_y(g):
                eng.wait_ge(pe_s[1], GRAPHS * (g.n + 1))
                wait(eng, pe_tail, at(TAIL_PE, g.n - 1, "lin1"))
                eng.activation(YS[:, :, :], pY[:, :], ACT.Copy).then_inc(act_y, 1)

            def negatives(g):
                eng.wait_ge(s_A[g.h], 16 * (g.half + 1))
                wait(eng, dve_least, g.n)
                eng.activation(unused[:, :, :], A[g.h][:, :, :], ACT.Relu, scale=-1.0, accum_out=least[:, :])\
                   .then_inc(act_least, 1)

            def body(g, nxt, prev, later, ended):
                def norm2(c):
                    eng.wait_ge(s_out, 16 * (c + 1))
                    tail_act(eng, c, "norm2")

                if not g:
                    copy_y(prev)
                    tail_act(eng, prev.n, "soft")
                    norm2(ended)
                    for stage in ("norm1", "spread"):
                        tail_act(eng, prev.n, stage)
                    norm2(prev.n)
                    return
                if prev:
                    copy_y(prev)
                if nxt:
                    copy_rf(nxt)
                soft(g, 1, 0)
                soft(g, 1, 1)
                squares(g, 2)
                if prev:
                    tail_act(eng, prev.n, "soft")

                soft(g, 2, 0)
                if nxt:
                    copy_listed(nxt, 0)
                soft(g, 2, 1)
                squares(g, 3)
                if nxt:
                    copy_listed(nxt, 1)
                negatives(g)

                soft(g, 3, 0)
                if nxt:
                    copy_listed(nxt, 2)
                soft(g, 3, 1)
                if nxt:
                    copy_listed(nxt, 3)
                if prev:
                    tail_act(eng, prev.n, "norm1")
                if ended is not None:
                    norm2(ended)

                if nxt:
                    copy_turned(nxt)
                if prev:
                    tail_act(eng, prev.n, "spread")
                if nxt:
                    squares(nxt, 0)
                    copy_list_rf(nxt, 0)
                eng.wait_ge(s_AR, 16 * (g.n + 1))
                for q in range(GRAPHS):
                    degree_act(eng, g.n, g.h, q)
                if nxt:
                    soft(nxt, 0, 0)
                    soft(nxt, 0, 1)
                    copy_list_rf(nxt, 1)
                    squares(nxt, 1)

            eng.preload_act_table_set("natural_log_exp_and_others")
            eng.wait_ge(s_const, 32)
            first = Group(0, 0, 0)
            copy_rf(first)
            eng.wait_ge(s_setup, 1)
            for k in range(LOOKS):
                copy_listed(first, k, (pW0, pW1)[k % 2])
            for l in range(LISTS):
                copy_list_rf(first, l, (pX0, pX1)[l])
            copy_turned(first)
            squares(first, 0)
            soft(first, 0, 0)
            soft(first, 0, 1)
            squares(first, 1)
            groups(eng, body)

            eng.wait_ge(s_verdict, 1)
            flagged = eng.value_load(verdict[0:1, 0:1])
            with eng.If(flagged != 0):
                with eng.Fori(0, dense_groups) as n:
                    eng.wait_ge(dn_rf, n + 1)
                    eng.activation(RF[0][:, :, LISTS, :], pM1[:, :].rearrange("p (a b) -> p a b", b=P), ACT.Copy)\
                       .then_inc(dn_rfc, 1)
                    with eng.Fori(0, GRAPHS * P // DENSE) as m:
                        k = n * (GRAPHS * P // DENSE) + m
                        eng.wait_ge(dn_pe, at(DENSE_PE, k, "turn"))
                        eng.activation(turned[:, :], pW0[:, 0:P], ACT.Copy).then_inc(dn_act, 1)
                        eng.wait_ge(dn_pe, at(DENSE_PE, k, "edge"))
                        some = slice(0, DENSE_PAIRS)
                        eng.activation(DIFF2[:, some, :], pE[:, 0:DENSE_PAIRS * P], ACT.Square, bias=NOFF)\
                           .then_inc(dn_act, 1)
                        eng.wait_ge(dn_act, at(DENSE_ACT, k, "square"))
                        eng.activation(G[:, some, :], DIFF2[:, some, :], ACT.Exp, scale=COEFF).then_inc(dn_act, 1)
                        eng.wait_ge(dn_dve, at(DENSE_DVE, k, "clamp"))
                        for i in (0, 1):
                            last = eng.activation(H[i][:, some, :], EX[i][:, some, :], ACT.Exp)
                        last.then_inc(dn_act, 1)
                        eng.wait_ge(dn_act, at(DENSE_ACT, k, "exp"))
                        for i in (0, 1):
                            last = eng.activation(EX[i][:, some, :], H[i][:, some, :], ACT.Ln, bias=halfc[:, :], scale=0.5)
                        last.then_inc(dn_act, 1)
                    eng.wait_ge(d_in, 64 * (n + 1))
                    for q in range(GRAPHS):
                        degree_act(eng, n + GROUPS, 0, q)
                    for stage in ("soft", "norm1", "spread", "norm2"):
                        tail_act(eng, n + GROUPS, stage)

        @block.vector
        def _(eng):
            def parts_of(value, exact, left_over, sem_, names, k):
                eng.tensor_copy(exact[0], value).then_inc(sem_, 1)
                eng.wait_ge(sem_, at(names, k, "hi"))
                eng.tensor_tensor(left_over, value, exact[0], ALU.subtract).then_inc(sem_, 1)
                eng.wait_ge(sem_, at(names, k, "rest"))
                eng.tensor_copy(exact[1], left_over).then_inc(sem_, 1)
                eng.wait_ge(sem_, at(names, k, "mid"))
                eng.tensor_tensor(exact[2], left_over, exact[1], ALU.subtract).then_inc(sem_, 1)

            def find_top(g, q):
                if q == 0:
                    eng.wait_ge(s_A[g.h], 16 * (g.half + 1))
                    eng.memset(spare[:, 0:1], 0.0)
                done = eng.max(top[:, q, :], A[g.h][:, q, :])
                if q == GRAPHS - 1:
                    done.then_inc(dve_prep, 1)

            def prep_direct(g, stage):
                eng.wait_ge(dve_prep, at(PREP_DVE, g.n, stage) - 1)
                if stage == "differ":
                    eng.tensor_tensor(differ[:, :, 1:DIRECT], top[:, :, 1:DIRECT], top[:, :, 0:DIRECT - 1],
                                      ALU.not_equal).then_inc(dve_prep, 1)
                if stage == "edge":
                    eng.tensor_tensor(edge[g.h][:, :, LISTS:SLOTS], top[:, :, 0:DIRECT], differ[:, :, :],
                                      ALU.mult).then_inc(dve_prep, 1)

            def left_below(g, i):
                eng.wait_ge(dve_prep, at(PREP_DVE, g.n, ("edge", "more1")[i]))
                above = more[:, :, TOP - 1:TOP] if i else top[:, :, DIRECT - 1:DIRECT]
                row = left if i else A[g.h]
                for q in range(GRAPHS):
                    last = eng.scalar_tensor_tensor(left[:, q, :], row[:, q, :], above[:, q, :], row[:, q, :],
                                                    ALU.is_lt, ALU.mult)
                last.then_inc(dve_prep, 1)

            def prep_more(g, i):
                eng.wait_ge(dve_prep, at(PREP_DVE, g.n, ("left1", "left2")[i]))
                eng.memset(spare[:, 1 + i:2 + i], 0.0)
                for q in range(GRAPHS):
                    last = eng.max(more[:, q, i * TOP:(i + 1) * TOP], left[:, q, :])
                last.then_inc(dve_prep, 1)

            def prep_lane(g):
                n, h = g.n, g.h
                eng.wait_ge(dve_prep, at(PREP_DVE, n, "more2"))
                eng.tensor_tensor(differ2[:, :, 1:MORE], more[:, :, 1:MORE], more[:, :, 0:MORE - 1],
                                  ALU.not_equal).then_inc(dve_prep, 1)
                eng.tensor_scalar(found[:, :, :], more[:, :, :], 0.0, None, ALU.is_gt).then_inc(dve_prep, 1)
                eng.tensor_tensor(flags[:, 0, :], flags[:, 0, :], more[:, :, MORE - 1], ALU.max)
                eng.wait_ge(dve_prep, at(PREP_DVE, n, "found"))
                wait(eng, pe_look, LOOKS * (n - 1))
                eng.tensor_tensor(rows[h][:, :, P:P + MORE], more[:, :, :], differ2[:, :, :], ALU.mult)\
                   .then_inc(dve_prep, 1)
                eng.reduce_sum(count[:, :], found[:, :, :], AX.X).then_inc(dve_prep, 1)

            def prep_starts(g):
                n, h = g.n, g.h
                eng.wait_ge(pe_base, n + 1)
                eng.tensor_copy(rows[h][:, :, P + MORE], pM1[:, 0:GRAPHS]).then_inc(dve_prep, 1)
                eng.tensor_tensor(span_end[:, :], pM1[:, 0:GRAPHS], count[:, :], ALU.add).then_inc(dve_prep, 1)

            def prep_started(g):
                n, h = g.n, g.h
                eng.wait_ge(dve_prep, at(PREP_DVE, n, "end"))
                for q in range(GRAPHS):
                    last = eng.tensor_scalar(started[:, q, :], iota[:, :], rows[h][:, q, P + MORE:ROW], None, ALU.is_ge)
                last.then_inc(dve_prep, 1)
                eng.scalar_tensor_tensor(flags[:, 1, :], span_end[:, :], float(LISTS * P), flags[:, 1, :],
                                         ALU.subtract, ALU.max)

            def prep_pick(g):
                n = g.n
                eng.wait_ge(dve_prep, at(PREP_DVE, n, "from"))
                wait(eng, pe_lrf, LISTS * n)
                for q in range(GRAPHS):
                    last = eng.scalar_tensor_tensor(pick[:, q, :], iota[:, :], span_end[:, q:q + 1], started[:, q, :],
                                                    ALU.is_lt, ALU.mult)
                last.then_inc(dve_prep, 1)

            def prep_parts(g, stage):
                n, h = g.n, g.h
                if stage == "place":
                    eng.wait_ge(act_look, LOOKS * (n + 1))
                    eng.tensor_tensor(place[:, :, :], place_of[:, :].unsqueeze(2).broadcast_to([P, LISTS, GRAPHS]),
                                      listed[h][:, :, :, P + MORE], ALU.subtract).then_inc(dve_prep, 1)
                else:
                    eng.wait_ge(dve_prep, at(PREP_DVE, n, stage) - 1)
                if stage == "match":
                    eng.tensor_tensor(match[:, :, :],
                                      iota[:, 0:MORE].unsqueeze(1).broadcast_to([P, LISTS * GRAPHS, MORE]),
                                      place.rearrange("p l q -> p (l q)").unsqueeze(2)
                                      .broadcast_to([P, LISTS * GRAPHS, MORE]), ALU.is_equal).then_inc(dve_prep, 1)
                if stage == "value":
                    eng.tensor_tensor(match[:, :, :], match[:, :, :],
                                      listed[h].rearrange("p l q r -> p (l q) r")[:, :, P:P + MORE], ALU.mult)\
                       .then_inc(dve_prep, 1)
                if stage == "listed":
                    for l in range(LISTS):
                        last = eng.reduce_sum(edge[h][:, :, l], match[:, l * GRAPHS:(l + 1) * GRAPHS, :],
                                              AX.X)
                    last.then_inc(dve_prep, 1)
                if stage == "hi":
                    wait(eng, pe_turn, n - 1)
                    eng.tensor_copy(parts[h][0], edge[h][:, :, :]).then_inc(dve_prep, 1)
                if stage == "rest":
                    eng.tensor_tensor(rest[:, :, :], edge[h][:, :, :], parts[h][0], ALU.subtract).then_inc(dve_prep, 1)
                if stage == "mid":
                    eng.tensor_copy(parts[h][1], rest[:, :, :]).then_inc(dve_prep, 1)
                if stage == "lo":
                    eng.tensor_tensor(parts[h][2], rest[:, :, :], parts[h][1], ALU.subtract).then_inc(dve_prep, 1)
                    eng.tensor_tensor(square[h][:, :, :], edge[h][:, :, :], edge[h][:, :, :], ALU.mult)\
                       .then_inc(dve_prep, 1)

            def hot_slot(g, q, s):
                if q == 0 and s == 0:
                    eng.wait_ge(dve_prep, at(PREP_DVE, g.n, "square"))
                if s == 0:
                    wait(eng, pe_s[1], GRAPHS * g.n + q - 1)
                row = listed[g.h][:, s, q, 0:P] if s < LISTS else A[g.h][:, q, :]
                done = eng.tensor_scalar(hot[q % 2][:, s, :], row, edge[g.h][:, q, s:s + 1],
                                         square[g.h][:, q, s:s + 1], ALU.is_equal, ALU.mult)
                if s == SLOTS - 1:
                    done.then_inc(dve_hot, 1)

            def hots(g, q):
                for s in range(SLOTS):
                    hot_slot(g, q, s)

            def message(g, q, i):
                u = GRAPHS * g.n + q
                if q == 0 and i == 0:
                    eng.wait_ge(act_lrf, LISTS * (g.n + 1))
                eng.wait_ge(pe_w[i], u + 1)
                wait(eng, pe_s[i], u)
                rf = RF[g.h][:, q, LISTS:LISTS + 1, :].broadcast_to([P, PAIRS, P]) if i else RF[g.h][:, q, :, :]
                eng.tensor_tensor(Z[i][:, :, :], (pW0, pW1)[i][:, 0:PAIRS * P].rearrange("p (a b) -> p a b", b=P),
                                  rf, ALU.mult).then_inc(dve_z[i], 1)

            def least_seen(g):
                eng.wait_ge(act_least, g.n + 1)
                eng.tensor_tensor(flags[:, 2, 0:1], flags[:, 2, 0:1], least[:, :], ALU.max).then_inc(dve_least, 1)

            def body(g, nxt, prev, later, ended):
                def tail(stage):
                    if prev:
                        tail_dve(eng, prev.n, prev.h, stage)

                if not g:
                    tail_dve(eng, ended, None, "shift2")
                    for stage in TAIL_DVE:
                        tail(stage)
                    return
                message(g, 0, 0)
                message(g, 0, 1)
                hot_slot(g, 1, 0)
                if nxt:
                    prep_starts(nxt)
                hot_slot(g, 1, 1)
                if nxt:
                    prep_started(nxt)
                hot_slot(g, 1, 2)
                if nxt:
                    prep_pick(nxt)
                for s in range(3, SLOTS):
                    hot_slot(g, 1, s)
                if ended is not None:
                    tail_dve(eng, ended, None, "shift2")

                message(g, 1, 0)
                hot_slot(g, 2, 0)
                message(g, 1, 1)
                hot_slot(g, 2, 1)
                tail("soft")
                for s in range(2, SLOTS):
                    hot_slot(g, 2, s)
                tail("sum1")
                hot_slot(g, 3, 0)
                tail("stats1")
                hot_slot(g, 3, 1)
                tail("moments1")

                message(g, 2, 0)
                message(g, 2, 1)
                least_seen(g)
                tail("shift1")
                for s, stage in zip(range(2, SLOTS), ("place", "match", "value", "listed")):
                    if nxt:
                        prep_parts(nxt, stage)
                    hot_slot(g, 3, s)
                if nxt:
                    for stage in ("hi", "rest", "mid", "lo"):
                        prep_parts(nxt, stage)

                message(g, 3, 0)
                message(g, 3, 1)
                if later:
                    for s in range(3):
                        hot_slot(nxt, 0, s)
                    for q in range(GRAPHS):
                        find_top(later, q)
                    hot_slot(nxt, 0, 3)
                    prep_direct(later, "differ")
                    hot_slot(nxt, 0, 4)
                    prep_direct(later, "edge")
                    hot_slot(nxt, 0, 5)
                    left_below(later, 0)
                    degree_dve(eng, g.n, g.h)
                    prep_more(later, 0)
                else:
                    degree_dve(eng, g.n, g.h)
                    if nxt:
                        hots(nxt, 0)
                tail("sum2")
                if later:
                    left_below(later, 1)
                tail("stats2")
                if later:
                    prep_more(later, 1)
                tail("moments2")
                if later:
                    prep_lane(later)

            eng.memset(flags[:, :, :], 0.0).then_inc(s_bound, 1)
            eng.memset(differ[:, :, :], 1.0)
            eng.memset(differ2[:, :, :], 1.0)
            for h in (0, 1):
                last = eng.memset(packed[h][:, :, :], 0.0)
            last.then_inc(s_bound, 1)
            eng.wait_ge(s_bound, 2)
            first = Group(0, 0, 0)
            for q in range(GRAPHS):
                find_top(first, q)
            prep_direct(first, "differ")
            prep_direct(first, "edge")
            for i in (0, 1):
                left_below(first, i)
                prep_more(first, i)
            prep_lane(first)
            prep_starts(first)
            prep_started(first)
            prep_pick(first)
            eng.wait_ge(s_setup, 1)
            eng.tensor_copy(choose[:, :, :], chosen.rearrange("r q p a -> r (q p a)").unsqueeze(2)
                            .broadcast_to([P, GRAPHS * PAIRS * 2, NG])).then_inc(s_setup, 1)
            eng.wait_ge(s_count, 1)
            eng.tensor_tensor(BD2X[:, :], pM0[:, 0:P], BD2R, ALU.add).then_inc(s_bd2x, 1)
            eng.wait_ge(s_const, 32)
            eng.tensor_scalar(B1L, B1, -LN2, None, ALU.add)
            eng.tensor_scalar(BD1N, BD1, -1.0, None, ALU.mult)
            eng.scalar_tensor_tensor(w1abs[:, :], W1, -1.0, W1, ALU.mult, ALU.max)
            eng.scalar_tensor_tensor(B1ABS, B1, -1.0, B1, ALU.mult, ALU.max).then_inc(s_bound, 1)
            eng.wait_ge(s_bound, 3)
            eng.reduce_sum(BOUND, w1abs[:, :], AX.X).then_inc(s_bound, 1)
            eng.wait_ge(s_bound, 4)
            eng.scalar_tensor_tensor(flags[:, 3, 0:1], BOUND, -SAFE, B1ABS, ALU.add, ALU.add)
            for stage in ("place", "match", "value", "listed", "hi", "rest", "mid", "lo"):
                prep_parts(first, stage)
            hots(first, 0)
            for q in range(GRAPHS):
                find_top(Group(1, 0, 1), q)
            prep_direct(Group(1, 0, 1), "differ")
            prep_direct(Group(1, 0, 1), "edge")
            for i in (0, 1):
                left_below(Group(1, 0, 1), i)
                prep_more(Group(1, 0, 1), i)
            prep_lane(Group(1, 0, 1))
            groups(eng, body)

            eng.wait_ge(dve_least, GROUPS)
            eng.reduce_max(worst[:, :], flags[:, :, :], AX.XY).then_inc(s_bound, 1)
            eng.wait_ge(s_bound, 5)
            eng.tensor_scalar(bad[:, :], worst[:, :], -1.0 if force_dense else 0.0, None, ALU.is_gt).then_inc(s_count, 1)
            eng.wait_ge(s_count, 3)
            eng.tensor_copy(verdict[:, :], pM1[0:1, 0:1]).then_inc(s_verdict, 1)
            eng.wait_ge(s_verdict, 1)
            flagged = eng.value_load(verdict[0:1, 0:1])
            with eng.If(flagged != 0):
                with eng.Fori(0, dense_groups) as n:
                    eng.wait_ge(dn_rfc, n + 1)
                    eng.memset(spare[:, 4:5], 0.0)
                    with eng.Fori(0, GRAPHS) as q:
                        with eng.Fori(0, P // DENSE) as t:
                            k = (n * GRAPHS + q) * (P // DENSE) + t
                            some, width = slice(0, DENSE_PAIRS), DENSE_PAIRS * P
                            eng.wait_ge(d_block, 16 * (k + 1))
                            eng.tensor_tensor(square[0][:, 0, 0:DENSE], VB[:, :], VB[:, :], ALU.mult)
                            exact = [x[:, 0, :].rearrange("r (a p) -> r a p", a=2)[:, :, 0:DENSE_PAIRS] for x in parts[0]]
                            parts_of(VB.rearrange("r (a p) -> r a p", a=2), exact,
                                     VR.rearrange("r (a p) -> r a p", a=2), dn_dve, DENSE_DVE, k)
                            eng.wait_ge(dn_pe, at(DENSE_PE, k, "lin1"))
                            for i, pX in enumerate((pX0, pX1)):
                                last = eng.tensor_scalar(EX[i][:, some, :], pX[:, 0:width], B1, SAFE, ALU.add, ALU.min)
                            last.then_inc(dn_dve, 1)
                            eng.wait_ge(dn_act, at(DENSE_ACT, k, "log"))
                            for i, pX in enumerate((pX0, pX1)):
                                last = eng.scalar_tensor_tensor(H[i][:, some, :], pX[:, 0:width], B1L, EX[i][:, some, :],
                                                                ALU.add, ALU.max)
                            last.then_inc(dn_dve, 1)
                            eng.wait_ge(dn_pe, at(DENSE_PE, k, "lin2"))
                            for i, pW in enumerate((pW0, pW1)):
                                last = eng.tensor_tensor(Z[i][:, some, :],
                                                         pW[:, 0:width].rearrange("p (a b) -> p a b", b=P),
                                                         B2R.unsqueeze(1).broadcast_to([P, DENSE_PAIRS, P]), ALU.add)
                            last.then_inc(dn_dve, 1)
                            eng.wait_ge(dn_dve, at(DENSE_DVE, k, "shift"))
                            rf = RF[0].rearrange("p a b c -> p (a b c)")[:, bass.ds(q * (LISTS + 1) * P + LISTS * P, P)]
                            for i in (0, 1):
                                last = eng.tensor_tensor(Z[i][:, some, :], Z[i][:, some, :],
                                                         rf.unsqueeze(1).broadcast_to([P, DENSE_PAIRS, P]), ALU.mult)
                            last.then_inc(dn_dve, 1)
                            eng.wait_ge(dn_pe, at(DENSE_PE, k, "y"))
                            eng.tensor_copy(YS.rearrange("p a b -> p (a b)")[:, bass.ds(q * P + t * DENSE, DENSE)],
                                            pY[:, 0:DENSE]).then_inc(dn_dve, 1)
                    eng.wait_ge(dn_dve, (n + 1) * (GRAPHS * P // DENSE) * len(DENSE_DVE))
                    eng.sem_inc(act_y, 1)
                    degree_dve(eng, n + GROUPS, 0)
                    for stage in TAIL_DVE:
                        tail_dve(eng, n + GROUPS, 0, stage)

        @block.gpsimd
        def _(eng):
            def squares(g):
                eng.wait_ge(s_A[g.h], 16 * (g.half + 1))
                wait(eng, pe_share, GRAPHS * (g.n - 1))
                eng.tensor_tensor(A2[g.h][:, :, :], A[g.h][:, :, :], A[g.h][:, :, :], ALU.mult).then_inc(pool_sq, 1)

            def rfb(g):
                eng.wait_ge(act_rf, g.n + 1)
                wait(eng, pe_share, GRAPHS * g.n)
                eng.tensor_tensor(RFB[:, :, :], RF[g.h][:, :, LISTS, :], B2R.unsqueeze(1).broadcast_to([P, GRAPHS, P]),
                                  ALU.mult).then_inc(pool_rfb, 1)

            def adj_eye(g):
                wait(eng, pe_tail, at(TAIL_PE, g.n - 2, "spread"))
                eng.tensor_tensor(AI[g.h][:, :, :], A[g.h][:, :, :], ident[:, :].unsqueeze(1).broadcast_to([P, GRAPHS, P]),
                                  ALU.add).then_inc(pool_ai, 1)

            def body(g, nxt, prev, later, ended):
                def tail(stage):
                    if prev:
                        if stage == "base":
                            eng.wait_ge(s_XN, 16 * (prev.n + 1))
                        tail_pool(eng, prev.n, prev.h, stage)

                if ended is not None:
                    tail_pool(eng, ended, None, "rstd2")
                tail("base")
                if g:
                    adj_eye(g)
                if nxt:
                    squares(nxt)
                tail("rstd1")
                tail("scaled")
                if nxt:
                    rfb(nxt)
                if g:
                    degree_pool(eng, g.n, g.h)
                if not g:
                    tail("rstd2")

            eng.memset(ones[:, :], 1.0)
            eng.memset(halfc[:, :], 0.5)
            eng.memset(chosen[:, :, :, :], 0.0).then_inc(s_pool, 1)
            eng.memset(minus_half[:, :], -0.5)
            eng.memset(epsilon[:, :], EPS)
            eng.memset(ident[:, :], 0.0).then_inc(s_pool, 1)
            eng.memset(before[:, :], 1.0).then_inc(s_pool, 1)
            eng.iota(iota[:, :], [[1, LISTS * P]], base=0, channel_multiplier=0, allow_small_or_imprecise_dtypes=True)
            eng.iota(place_of[:, :], [[P, LISTS]], base=0, channel_multiplier=1, allow_small_or_imprecise_dtypes=True)
            eng.wait_ge(s_pool, 3)
            eng.affine_select(out=ident[:, :], in_=ident[:, :], compare_op=ALU.not_equal, fill=1.0,
                              base=0, pattern=[[-1, P]], channel_multiplier=1).then_inc(s_pool, 1)
            eng.affine_select(out=before[:, :], in_=before[:, :], compare_op=ALU.is_gt, fill=0.0,
                              base=0, pattern=[[1, P]], channel_multiplier=-1)
            for i in range(3):
                eng.wait_ge(s_pool, 3 + i + (i > 0))
                eng.affine_select(out=chosen[:, :, :, :], in_=chosen[:, :, :, :], compare_op=ALU.not_equal, fill=1.0,
                                  base=-SLOTS * i, pattern=[[-BLOCK, GRAPHS], [-1, PAIRS], [-PAIRS, 2]],
                                  channel_multiplier=1).then_inc(s_pool, 1)
            eng.wait_ge(s_pool, 7)
            eng.tensor_copy(identb[:, :], ident[:, :]).then_inc(s_setup, 1)
            eng.wait_ge(s_const, 32)
            squares(Group(0, 0, 0))
            eng.wait_ge(s_bd2x, 1)
            rfb(Group(0, 0, 0))
            groups(eng, body)

            eng.wait_ge(s_verdict, 1)
            flagged = eng.value_load(verdict[0:1, 0:1])
            with eng.If(flagged != 0):
                with eng.Fori(0, dense_groups) as n:
                    eng.wait_ge(d_in, 64 * (n + 1))
                    eng.tensor_tensor(AI[0][:, :, :], A[0][:, :, :], ident[:, :].unsqueeze(1).broadcast_to([P, GRAPHS, P]),
                                      ALU.add).then_inc(dn_ai, 1)
                    degree_pool(eng, n + GROUPS, 0)
                    for stage in ("base", "rstd1", "scaled", "rstd2"):
                        tail_pool(eng, n + GROUPS, 0, stage)


def kernel(**inputs):
    import concourse.bacc as bacc
    from concourse.bass_utils import run_bass_kernel_spmd

    def by_node(a):
        return np.ascontiguousarray(a).reshape(P, B * P)

    i = {k: np.asarray(v) for k, v in inputs.items()}
    offsets = -np.linspace(0.0, CUTOFF, NG, dtype=np.float32)
    w1T = i["L0_gnn_W1"].T
    arrays = {
        "adjT": by_node(i["adj"].transpose(2, 0, 1)),
        "adj_rows": by_node(i["adj"].transpose(1, 0, 2)),
        "x_nodes": by_node(i["x"].transpose(1, 0, 2)),
        "x_features": by_node(i["x"].transpose(2, 0, 1)),
        "weights": np.ascontiguousarray(np.concatenate([
            np.concatenate([w1T, w1T]), i["L0_gnn_W2"].T, i["L0_gnn_Wa"].T, i["L0_gnn_Wd1"].T, i["L0_gnn_Wd2"].T,
            i["L1_gnn_weight"], i["L0_gnn_W1"], i["L0_gnn_b1"][:, None], i["L0_gnn_bd1"][:, None],
            np.concatenate([offsets, offsets])[:, None]], axis=1)),
        "biases": np.concatenate([i["L0_gnn_b2"], i["L0_gnn_bd2"], i["L1_gnn_bias"]]).reshape(1, 3 * P),
    }
    nc = bacc.Bacc("TRN2", target_bir_lowering=False, num_devices=1)
    args = [nc.dram_tensor(n, a.shape, mybir.dt.from_np(a.dtype), kind="ExternalInput").ap() for n, a in arrays.items()]
    out = nc.dram_tensor("out_nodes", (P, B * P), mybir.dt.float32, kind="ExternalOutput").ap()
    gnn_kernel(nc, *args, out)
    r = run_bass_kernel_spmd(nc, [arrays], core_ids=[0])
    return np.ascontiguousarray(r.results[0]["out_nodes"].reshape(P, B, P).transpose(1, 0, 2))
```
